# Optimizing a Trainium2 kernel written in Bass

```python
import numpy as np
import jax
import jax.numpy as jnp

def _softmax(x, axis=-1):
    return jax.nn.softmax(x, axis=axis)

def _gelu(x):
    return jax.nn.gelu(x, approximate=True)

def _silu(x):
    return jax.nn.silu(x)

def _sigmoid(x):
    return jax.nn.sigmoid(x)

def _layernorm(x, axis=-1, eps=1e-05):
    m = jnp.mean(x, axis=axis, keepdims=True)
    v = jnp.var(x, axis=axis, keepdims=True)
    return (x - m) / jnp.sqrt(v + eps)

def _scatter_add(tgt, idx, src, axis=0):
    return tgt.at[idx].add(src)

def _segment_sum(src, seg, n):
    return jax.ops.segment_sum(src, seg, n)
kernel_name = 'mk_vit_tower_d1_tok_img768_r4_279f06'

def setup_inputs(seed: int=0):
    np.random.seed(seed)
    _w = jnp.asarray

    def _rec_inputs():
        import jax
        import jax.numpy as jnp
        _rk = jax.random.key(seed)
        x = -0.000596345 + 1.00056 * jax.random.normal(jax.random.fold_in(_rk, 1), (16, 3, 64, 64), jnp.float32)
        return x
    x = _rec_inputs()

    def _L0_tok_setup():
        import jax, jax.numpy as jnp
        import numpy as np
        B = 16
        IMG = 64
        CH = 3
        EMBED = 64
        GP = 16
        PRE = [1, 2, 4]
        N_LEVELS = 3
        FUSED = EMBED * N_LEVELS

        def hilbert_flat_indices(n):
            t = np.arange(n * n, dtype=np.int64)
            x = np.zeros(n * n, dtype=np.int64)
            y = np.zeros(n * n, dtype=np.int64)
            s = 1
            while s < n:
                rx = 1 & t // 2
                ry = 1 & (t ^ rx)
                swap = ry == 0
                flip = swap & (rx == 1)
                x = np.where(flip, s - 1 - x, x)
                y = np.where(flip, s - 1 - y, y)
                x2 = np.where(swap, y, x)
                y2 = np.where(swap, x, y)
                x, y = (x2, y2)
                x = x + s * rx
                y = y + s * ry
                t = t // 4
                s *= 2
            return y * n + x

        def _level(x, idx, W, b, p, gp):
            Bsz, C, H, _ = x.shape
            h = H // p
            t = x.reshape(Bsz, C, h, p, h, p).transpose(0, 2, 4, 3, 5, 1).reshape(Bsz, h * h, p * p * C)
            t = t[:, idx]
            t = t.reshape(Bsz, h * h // gp, gp * p * p * C)
            return t @ W.T + b

        def _interp_linear(x, n_out):
            L = x.shape[1]
            pos = (jnp.arange(n_out, dtype=jnp.float32) + 0.5) * (L / n_out) - 0.5
            pos = jnp.clip(pos, 0.0, L - 1)
            i0 = jnp.floor(pos).astype(jnp.int32)
            i1 = jnp.minimum(i0 + 1, L - 1)
            w = (pos - i0).astype(x.dtype)
            return x[:, i0] * (1.0 - w)[None, :, None] + x[:, i1] * w[None, :, None]
        key = jax.random.key(seed)
        ks = jax.random.split(key, 9)
        inp = {'x': jax.random.normal(ks[0], (B, CH, IMG, IMG), jnp.float32)}
        for i, p in enumerate(PRE):
            din = CH * p * p * GP
            inp[f'W{i}'] = jax.random.normal(ks[1 + 2 * i], (EMBED, din), jnp.float32) * din ** (-0.5)
            inp[f'b{i}'] = jax.random.normal(ks[2 + 2 * i], (EMBED,), jnp.float32) * 0.02
        inp['Wf'] = jax.random.normal(ks[7], (FUSED, FUSED), jnp.float32) * FUSED ** (-0.5)
        inp['bf'] = jax.random.normal(ks[8], (FUSED,), jnp.float32) * 0.02
        for i, p in enumerate(PRE):
            inp[f'idx{i}'] = jnp.asarray(hilbert_flat_indices(IMG // p), jnp.int32)
        return inp
    _L0_tok_all = _L0_tok_setup()
    _L0_tok_in = {k: v for k, v in _L0_tok_all.items() if k in ('W0', 'b0', 'W1', 'b1', 'W2', 'b2', 'Wf', 'bf', 'idx0', 'idx1', 'idx2')}
    del _L0_tok_all

    def _L0_attn_setup():
        import jax, jax.numpy as jnp
        import numpy as np
        NUM_HEADS = 12
        LN_EPS = 1e-05
        key = jax.random.key(seed)
        k1, k2, k3 = jax.random.split(key, 3)
        B, S, E = (8, 256, 192)
        x = jax.random.normal(k1, (B, S, E), dtype=jnp.float32)
        w_qkv = jax.random.normal(k2, (E, 3 * E), dtype=jnp.float32) * (1.0 / np.sqrt(E))
        b_qkv = jax.random.normal(k3, (3 * E,), dtype=jnp.float32) * 0.02
        ln_gamma = jnp.ones((E,), dtype=jnp.float32)
        ln_beta = jnp.zeros((E,), dtype=jnp.float32)
        return {'x': x, 'w_qkv': w_qkv, 'b_qkv': b_qkv, 'ln_gamma': ln_gamma, 'ln_beta': ln_beta}
    _L0_attn_all = _L0_attn_setup()
    _L0_attn_in = {k: v for k, v in _L0_attn_all.items() if k in ('w_qkv', 'b_qkv', 'ln_gamma', 'ln_beta')}
    del _L0_attn_all

    def _L0_ffn_setup():
        import jax, jax.numpy as jnp
        import numpy as np
        E = 192
        H = 12
        D = E // H
        HID = 768
        NEXP = 4
        TOPK = 2
        EPS = 1e-05

        def _ln(x, g, b):
            m = jnp.mean(x, axis=-1, keepdims=True)
            v = jnp.mean(jnp.square(x - m), axis=-1, keepdims=True)
            return (x - m) * jax.lax.rsqrt(v + EPS) * g + b
        key = jax.random.key(seed)
        ks = jax.random.split(key, 10)
        s = 0.02
        return {'x': jax.random.normal(ks[0], (8, 256, E), jnp.float32), 'ln1_g': jnp.ones((E,), jnp.float32), 'ln1_b': jnp.zeros((E,), jnp.float32), 'in_w': jax.random.normal(ks[1], (3 * E, E), jnp.float32) * s, 'in_b': jnp.zeros((3 * E,), jnp.float32), 'out_w': jax.random.normal(ks[2], (E, E), jnp.float32) * s, 'out_b': jnp.zeros((E,), jnp.float32), 'mlp_w1': jax.random.normal(ks[3], (E, HID), jnp.float32) * s, 'mlp_b1': jnp.zeros((HID,), jnp.float32), 'mlp_w2': jax.random.normal(ks[4], (HID, E), jnp.float32) * s, 'mlp_b2': jnp.zeros((E,), jnp.float32), 'ln2_g': jnp.ones((E,), jnp.float32), 'ln2_b': jnp.zeros((E,), jnp.float32), 'gate_w': jax.random.normal(ks[5], (NEXP, E), jnp.float32) * s, 'gate_b': jnp.zeros((NEXP,), jnp.float32), 'exp_w1': jax.random.normal(ks[6], (NEXP, E, HID), jnp.float32) * s, 'exp_b1': jnp.zeros((NEXP, HID), jnp.float32), 'exp_w2': jax.random.normal(ks[7], (NEXP, HID, E), jnp.float32) * s, 'exp_b2': jnp.zeros((NEXP, E), jnp.float32)}
    _L0_ffn_all = _L0_ffn_setup()
    _L0_ffn_in = {k: v for k, v in _L0_ffn_all.items() if k in ('ln1_g', 'ln1_b', 'in_w', 'in_b', 'out_w', 'out_b', 'mlp_w1', 'mlp_b1', 'mlp_w2', 'mlp_b2', 'ln2_g', 'ln2_b', 'gate_w', 'gate_b', 'exp_w1', 'exp_b1', 'exp_w2', 'exp_b2')}
    del _L0_ffn_all
    return {'x': x, 'L0_tok_W0': _L0_tok_in['W0'], 'L0_tok_b0': _L0_tok_in['b0'], 'L0_tok_W1': _L0_tok_in['W1'], 'L0_tok_b1': _L0_tok_in['b1'], 'L0_tok_W2': _L0_tok_in['W2'], 'L0_tok_b2': _L0_tok_in['b2'], 'L0_tok_Wf': _L0_tok_in['Wf'], 'L0_tok_bf': _L0_tok_in['bf'], 'L0_tok_idx0': _L0_tok_in['idx0'], 'L0_tok_idx1': _L0_tok_in['idx1'], 'L0_tok_idx2': _L0_tok_in['idx2'], 'L0_attn_w_qkv': _L0_attn_in['w_qkv'], 'L0_attn_b_qkv': _L0_attn_in['b_qkv'], 'L0_attn_ln_gamma': _L0_attn_in['ln_gamma'], 'L0_attn_ln_beta': _L0_attn_in['ln_beta'], 'L0_ffn_ln1_g': _L0_ffn_in['ln1_g'], 'L0_ffn_ln1_b': _L0_ffn_in['ln1_b'], 'L0_ffn_in_w': _L0_ffn_in['in_w'], 'L0_ffn_in_b': _L0_ffn_in['in_b'], 'L0_ffn_out_w': _L0_ffn_in['out_w'], 'L0_ffn_out_b': _L0_ffn_in['out_b'], 'L0_ffn_mlp_w1': _L0_ffn_in['mlp_w1'], 'L0_ffn_mlp_b1': _L0_ffn_in['mlp_b1'], 'L0_ffn_mlp_w2': _L0_ffn_in['mlp_w2'], 'L0_ffn_mlp_b2': _L0_ffn_in['mlp_b2'], 'L0_ffn_ln2_g': _L0_ffn_in['ln2_g'], 'L0_ffn_ln2_b': _L0_ffn_in['ln2_b'], 'L0_ffn_gate_w': _L0_ffn_in['gate_w'], 'L0_ffn_gate_b': _L0_ffn_in['gate_b'], 'L0_ffn_exp_w1': _L0_ffn_in['exp_w1'], 'L0_ffn_exp_b1': _L0_ffn_in['exp_b1'], 'L0_ffn_exp_w2': _L0_ffn_in['exp_w2'], 'L0_ffn_exp_b2': _L0_ffn_in['exp_b2']}

def reference(x, L0_tok_W0, L0_tok_b0, L0_tok_W1, L0_tok_b1, L0_tok_W2, L0_tok_b2, L0_tok_Wf, L0_tok_bf, L0_tok_idx0, L0_tok_idx1, L0_tok_idx2, L0_attn_w_qkv, L0_attn_b_qkv, L0_attn_ln_gamma, L0_attn_ln_beta, L0_ffn_ln1_g, L0_ffn_ln1_b, L0_ffn_in_w, L0_ffn_in_b, L0_ffn_out_w, L0_ffn_out_b, L0_ffn_mlp_w1, L0_ffn_mlp_b1, L0_ffn_mlp_w2, L0_ffn_mlp_b2, L0_ffn_ln2_g, L0_ffn_ln2_b, L0_ffn_gate_w, L0_ffn_gate_b, L0_ffn_exp_w1, L0_ffn_exp_b1, L0_ffn_exp_w2, L0_ffn_exp_b2):
    import jax
    import jax.numpy as jnp

    def _L0_tok_ref(x, W0, b0, W1, b1, W2, b2, Wf, bf, idx0, idx1, idx2):
        import jax, jax.numpy as jnp
        import numpy as np
        B = 16
        IMG = 64
        CH = 3
        EMBED = 64
        GP = 16
        PRE = [1, 2, 4]
        N_LEVELS = 3
        FUSED = EMBED * N_LEVELS

        def hilbert_flat_indices(n):
            t = np.arange(n * n, dtype=np.int64)
            x = np.zeros(n * n, dtype=np.int64)
            y = np.zeros(n * n, dtype=np.int64)
            s = 1
            while s < n:
                rx = 1 & t // 2
                ry = 1 & (t ^ rx)
                swap = ry == 0
                flip = swap & (rx == 1)
                x = np.where(flip, s - 1 - x, x)
                y = np.where(flip, s - 1 - y, y)
                x2 = np.where(swap, y, x)
                y2 = np.where(swap, x, y)
                x, y = (x2, y2)
                x = x + s * rx
                y = y + s * ry
                t = t // 4
                s *= 2
            return y * n + x

        def _level(x, idx, W, b, p, gp):
            Bsz, C, H, _ = x.shape
            h = H // p
            t = x.reshape(Bsz, C, h, p, h, p).transpose(0, 2, 4, 3, 5, 1).reshape(Bsz, h * h, p * p * C)
            t = t[:, idx]
            t = t.reshape(Bsz, h * h // gp, gp * p * p * C)
            return t @ W.T + b

        def _interp_linear(x, n_out):
            L = x.shape[1]
            pos = (jnp.arange(n_out, dtype=jnp.float32) + 0.5) * (L / n_out) - 0.5
            pos = jnp.clip(pos, 0.0, L - 1)
            i0 = jnp.floor(pos).astype(jnp.int32)
            i1 = jnp.minimum(i0 + 1, L - 1)
            w = (pos - i0).astype(x.dtype)
            return x[:, i0] * (1.0 - w)[None, :, None] + x[:, i1] * w[None, :, None]
        Ws = [(idx0, W0, b0, PRE[0]), (idx1, W1, b1, PRE[1]), (idx2, W2, b2, PRE[2])]
        outs = [_level(x, idx, W, b, p, GP) for idx, W, b, p in Ws]
        n_tokens = outs[0].shape[1]
        outs = [outs[0]] + [_interp_linear(o, n_tokens) for o in outs[1:]]
        y = jnp.concatenate(outs, axis=-1)
        return y @ Wf.T + bf

    def _L0_attn_ref(x, w_qkv, b_qkv, ln_gamma, ln_beta):
        import jax, jax.numpy as jnp
        import numpy as np
        NUM_HEADS = 12
        LN_EPS = 1e-05
        B, S, E = x.shape
        H = NUM_HEADS
        D = E // H
        qkv = x @ w_qkv + b_qkv
        qkv = qkv.reshape(B, S, 3, H, D)
        q, k, v = (qkv[:, :, 0], qkv[:, :, 1], qkv[:, :, 2])
        scores = jnp.einsum('bshd,bthd->bhst', q, k) / jnp.sqrt(jnp.float32(D))
        attn = jax.nn.softmax(scores, axis=-1)
        out = jnp.einsum('bhst,bthd->bshd', attn, v)
        out = out.reshape(B, S, E)
        y = x + out
        mean = jnp.mean(y, axis=-1, keepdims=True)
        var = jnp.var(y, axis=-1, keepdims=True)
        y = (y - mean) * jax.lax.rsqrt(var + LN_EPS)
        return y * ln_gamma + ln_beta

    def _L0_ffn_ref(x, ln1_g, ln1_b, in_w, in_b, out_w, out_b, mlp_w1, mlp_b1, mlp_w2, mlp_b2, ln2_g, ln2_b, gate_w, gate_b, exp_w1, exp_b1, exp_w2, exp_b2):
        import jax, jax.numpy as jnp
        import numpy as np
        E = 192
        H = 12
        D = E // H
        HID = 768
        NEXP = 4
        TOPK = 2
        EPS = 1e-05

        def _ln(x, g, b):
            m = jnp.mean(x, axis=-1, keepdims=True)
            v = jnp.mean(jnp.square(x - m), axis=-1, keepdims=True)
            return (x - m) * jax.lax.rsqrt(v + EPS) * g + b
        B, N, _ = x.shape
        h = _ln(x, ln1_g, ln1_b)
        qkv = h @ in_w.T + in_b
        q, k, v = jnp.split(qkv, 3, axis=-1)
        q = q.reshape(B, N, H, D)
        k = k.reshape(B, N, H, D)
        v = v.reshape(B, N, H, D)
        scores = jnp.einsum('bqhd,bkhd->bhqk', q, k) / jnp.sqrt(jnp.float32(D))
        attn = jax.nn.softmax(scores, axis=-1)
        ctx = jnp.einsum('bhqk,bkhd->bqhd', attn, v).reshape(B, N, E)
        x = x + ctx @ out_w.T + out_b
        x = x + jax.nn.gelu(x @ mlp_w1 + mlp_b1, approximate=False) @ mlp_w2 + mlp_b2
        xm = _ln(x, ln2_g, ln2_b)
        logits = xm @ gate_w.T + gate_b
        topv, topi = jax.lax.top_k(logits, TOPK)
        gates = jax.nn.softmax(topv, axis=-1)
        onehot = jax.nn.one_hot(topi, NEXP, dtype=x.dtype)
        comb = jnp.einsum('bnk,bnke->bne', gates, onehot)
        moe_out = jnp.zeros_like(x)
        for e in range(NEXP):
            he = jax.nn.gelu(xm @ exp_w1[e] + exp_b1[e], approximate=False)
            oe = he @ exp_w2[e] + exp_b2[e]
            moe_out = moe_out + comb[..., e:e + 1] * oe
        return x + moe_out
    h = _L0_tok_ref(x, L0_tok_W0, L0_tok_b0, L0_tok_W1, L0_tok_b1, L0_tok_W2, L0_tok_b2, L0_tok_Wf, L0_tok_bf, L0_tok_idx0, L0_tok_idx1, L0_tok_idx2)
    h = h + _L0_attn_ref(_layernorm(h, axis=-1), L0_attn_w_qkv, L0_attn_b_qkv, L0_attn_ln_gamma, L0_attn_ln_beta)
    h = h + _L0_ffn_ref(_layernorm(h, axis=-1), L0_ffn_ln1_g, L0_ffn_ln1_b, L0_ffn_in_w, L0_ffn_in_b, L0_ffn_out_w, L0_ffn_out_b, L0_ffn_mlp_w1, L0_ffn_mlp_b1, L0_ffn_mlp_w2, L0_ffn_mlp_b2, L0_ffn_ln2_g, L0_ffn_ln2_b, L0_ffn_gate_w, L0_ffn_gate_b, L0_ffn_exp_w1, L0_ffn_exp_b1, L0_ffn_exp_w2, L0_ffn_exp_b2)
    return h

_drawn_inputs = setup_inputs


def setup_inputs(seed=0):
    import zlib

    import numpy as np

    out = dict(_drawn_inputs(seed))
    spreads = {'L0_attn_ln_gamma': (1.0, 0.2),
     'L0_attn_ln_beta': (0.0, 0.1),
     'L0_ffn_ln1_g': (1.0, 0.6),
     'L0_ffn_ln1_b': (0.0, 0.8),
     'L0_ffn_in_b': (0.0, 0.8),
     'L0_ffn_out_b': (0.0, 0.485),
     'L0_ffn_mlp_b1': (0.0, 0.647),
     'L0_ffn_mlp_b2': (0.0, 0.427),
     'L0_ffn_ln2_g': (1.0, 0.6),
     'L0_ffn_ln2_b': (0.0, 0.8),
     'L0_ffn_gate_b': (0.0, 0.489),
     'L0_ffn_exp_b1': (0.0, 0.8),
     'L0_ffn_exp_b2': (0.0, 0.34)}
    factors = {'L0_tok_b0': 4.294,
     'L0_tok_b1': 4.128,
     'L0_tok_b2': 3.506,
     'L0_attn_b_qkv': 4.923,
     'L0_ffn_in_w': 7.986,
     'L0_ffn_out_w': 4.641,
     'L0_ffn_gate_w': 2.758,
     'L0_ffn_exp_w1': 2.811}
    for name, (base, spread) in spreads.items():
        noise = np.random.default_rng([zlib.crc32(name.encode()), seed]).standard_normal(out[name].shape)
        drawn = base * np.exp(spread * noise) if base else spread * noise
        out[name] = jnp.asarray(drawn.astype(out[name].dtype))
    for name, factor in factors.items():
        out[name] = (out[name] * factor).astype(out[name].dtype)
    return out
```

```python
from contextlib import ExitStack

import concourse.bass as bass
import numpy as np
from concourse import mybir

F32 = mybir.dt.float32
F32R = mybir.dt.float32r
I32 = mybir.dt.int32
ALU = mybir.AluOpType
ACT = mybir.ActivationFunctionType
AX = mybir.AxisListType

P = 128
B, CH, IMG = 16, 3, 64
GP = 16
PRE = (1, 2, 4)
N = IMG * IMG // GP
L1, L2 = N // 4, N // 16
C0, C1, C2 = (CH * p * p for p in PRE)
EMB = 64
E = 3 * EMB
E2 = E - P
H, D = 12, 16
HP = H // 2
DS = 64
HID = 768
MT = HID // P
NEXP = 4
NMLP = 1 + NEXP
EPS = 1e-5
PAIR = 2
T = PAIR * N
NBLK = T // P
NIT = B // PAIR
MAGIC = float(0x5F3759DF)
NEWTON = 3
BIAS_AT = (0, 32, 64)


def ev(i, per, n):
    return (i + 1) * per + n + 1


class Ring:

    def __init__(self, products, full, read):
        self.full_sem, self.read_sem = full, read
        self.slot = {name: k % len(full) for k, name in enumerate(products)}
        self.nth = {name: k // len(full) for k, name in enumerate(products)}
        self.per = [sum(s == k for s in self.slot.values()) for k in range(len(full))]

    def full(self, i, name):
        s = self.slot[name]
        return self.full_sem[s], ev(i, self.per[s], self.nth[name])

    def read(self, i, name):
        s = self.slot[name]
        return self.read_sem[s], ev(i, self.per[s], self.nth[name])

    def room(self, i, name):
        s = self.slot[name]
        return self.read_sem[s], ev(i, self.per[s], self.nth[name] - 1)



def ring_products():
    def prepare(a, b):
        return [("qk", a, b, 0), ("qk", a, b, 1), ("v", a, b)] + [(x, a, b, g) for x in "kq" for g in range(3)]

    out = []
    for a in range(2):
        out += [("split_a", a), ("split_c", a)] + prepare(a, 0)
        out += [("max", a, 0, n) for n in range(12)] + prepare(a, 1) + [("negmax", a, 0)]
        for n in range(12 + LAG):
            out += [("max", a, 1, n)] * (n < 12) + [("score", a, 0, n - LAG)] * (n >= LAG)
            out += [("negmax", a, 1)] * (n == NEG_AT + LAG)
        out += [("ctx", a, 0, 0), ("ctx", a, 0, 1)]
        out += [("score", a, 1, n) for n in range(12)] + [("ctx", a, 1, 0), ("ctx", a, 1, 1)]
    return out + [("ctxT", 0), ("ctxT", 1), ("proj", 0), ("proj", 1)]


def hid_products():
    out = [("split_a", 2), ("split_c", 2)] + [("up", c) for c in range(MT)]
    return out + [("split_a", 3), ("split_c", 3), ("gate",)] + [("up", c) for c in range(MT, MT * NMLP)]


def prepare_and_tokenize(nc, a, keep, const):
    with ExitStack() as ctx:
        sb = lambda name, shape, dt=F32: ctx.enter_context(nc.sbuf_tensor(name, shape, dt))
        sem = lambda name: ctx.enter_context(nc.semaphore(name))
        bank = [ctx.enter_context(nc.psum_tensor(f"tok_bank{k}", [P, 512], F32)) for k in range(8)]

        ident = keep["ident"]
        idx0 = sb("idx0", [P, 2, GP], I32)
        idx1 = sb("idx1", [P, 8], I32)
        idx2 = sb("idx2", [P, 2], I32)
        g0 = sb("g0", [P, 2, GP, B * C0])
        g12 = sb("g12", [P, 2 * 8 * B * C1])
        g1 = g12[:, 0:8 * B * C1].rearrange("p (m n) -> p m n", m=8)
        g2 = g12[:, 8 * B * C1:].rearrange("p (m n) -> p m n", m=2)
        x1T = g12[0:96, 0:2 * B * L1].rearrange("p (q n) -> p q n", q=2)
        x2T = g12[:, 8 * B * C1:].rearrange("p (q n) -> p q n", q=6)
        x1 = sb("x1tok", [P, 8, GP * C1])
        x2 = sb("x2tok", [P, 2, GP * C2])
        x0T = sb("x0T", [GP * C0, 2, 512])
        y0I = sb("y0I", [P, B * P])
        y1T = sb("y1T", [EMB, B * L1])
        y2T = sb("y2T", [EMB, B * L2])
        wfa = sb("wfa", [P, B, E])
        a2 = sb("a2", [P, 2, E])
        int2 = sb("int2", [P, 2, N])
        w0T = sb("w0T", [GP * C0, EMB])
        w1T = sb("w1T", [96, 2, EMB])
        w2T = sb("w2T", [P, 6, EMB])
        wfT = sb("wfT", [EMB, 3, E])
        tb = sb("tb", [EMB, 3])
        bfb = sb("bfb", [P, E])
        HB = 3
        hout = sb("hout", [P, HB, 2, E])
        raw = sb("raw", [P, 2, MT * E])
        rawc = sb("rawc", [P, 2, HID])

        idx_in, misc_in = sem("idx_in"), sem("misc_in")
        gathered0, gathered1, gathered2 = [sem("gathered0a"), sem("gathered0b")], sem("gathered1"), sem("gathered2")
        scratch_out, x1_in, x2_in, interp_in = sem("scratch_out"), sem("x1_in"), sem("x2_in"), sem("interp_in")
        hi_done, lo_done = sem("hi_done"), sem("lo_done")
        ident0, ident_done = sem("ident0"), sem("ident_done")
        tr_done, tr_evac = sem("tr_done"), sem("tr_evac")
        h_out = [sem(f"h_out{k}") for k in range(HB)]
        rows_in, rows_done, ones_done, row_out = sem("rows_in"), sem("rows_done"), sem("ones_done"), sem("row_out")
        block = ctx.enter_context(nc.Block())

        s1, s2 = const["scratch1"], const["scratch2"]

        pieces = []
        for l in range(2):
            pieces.append(("wide", a["wqkv"][l, 0:P, :], keep["wq_h"][:, l, :], keep["wq_l"][:, l, :], 3 * E))
            pieces.append(("tail", a["wqkv"][l, P:E, :], keep["wq_c"][:, l, :], None, 3 * E))
        pieces.append(("wide", a["gate_wT"][0:P, :], keep["gw_h"][:, :], keep["gw_l"][:, :], NEXP))
        pieces.append(("tail", a["gate_wT"][P:E, :], keep["gw_c"][:, :], None, NEXP))
        for e in range(NMLP):
            pieces.append(("wide", a["w1"][e, 0:P, :], keep["w1_h"][:, e, :], keep["w1_l"][:, e, :], HID))
            pieces.append(("tail", a["w1"][e, P:E, :], keep["w1_c"][:, e, :], None, HID))
            pieces.append(("wide", a["w2"][:, e, :], keep["w2_h"][:, e, :], keep["w2_l"][:, e, :], MT * E))
        stage = []
        for k, (kind, _, _, _, n) in enumerate(pieces):
            t = raw if kind == "wide" else rawc
            stage.append(t[:, sum(pieces[j][0] == kind for j in range(k)) % 2, 0:n])
        before = []
        for k, (kind, *_) in enumerate(pieces):
            same = [j for j in range(k) if pieces[j][0] == kind]
            before.append(same[-2] if len(same) >= 2 else None)
        raws = [sem(f"raw_{k}") for k in range(4)]
        part, turn = [], {}
        for k, (kind, *_) in enumerate(pieces):
            c = (kind == "tail") * 2 + sum(pieces[j][0] == kind for j in range(k)) % 2
            turn[c] = turn.get(c, 0) + (16 if kind == "wide" else 32)
            part.append((raws[c], turn[c]))

        rb = keep["bias"]
        bias_rows = [(rb[q:q + 2, 0:3 * E], a["bqkv"][l:l + 1, :], y0I[q:q + 1, 0:3 * E])
                     for l, q in enumerate(BIAS_AT[:2])]
        bias_rows.append((rb[0:2, 3 * E:4 * E], a["ob"], y0I[0:1, 3 * E:4 * E]))
        q = BIAS_AT[2]
        hrow = hout[q:q + 1].rearrange("p a b c -> p (a b c)")
        bias_rows += [(rb[q:q + 2, 0:NMLP * E], a["b2"], hrow[:, 0:NMLP * E]),
                      (rb[q:q + 2, NMLP * E:], a["gate_b"], hrow[:, NMLP * E:NMLP * E + NEXP])]

        steps = ([("x2T", c) for c in range(3)] + [("y2", 0)] + [("x1T", c) for c in range(4)]
                 + [("y1", c) for c in range(2)] + [("a2", 0)] + [("a1", c) for c in range(8)])
        for half in range(2):
            for c in range(4):
                steps += [("x0T", half, c), ("y0", half, c)]
            steps += [("h", half, c) for c in range(8)]
        order = {s: n for n, s in enumerate(steps)}

        @block.sync
        def _(sp):
            sp.dma_start(idx2[:, :], a["idx2"]).then_inc(idx_in, 16)
            sp.dma_start(idx1[:, :], a["idx1"]).then_inc(idx_in, 16)
            sp.dma_start(idx0[:, :, :], a["idx0"]).then_inc(idx_in, 16)
            for _, src, row in bias_rows:
                sp.dma_start(row, src).then_inc(rows_in, 16)
            for dst, src in ((w0T[:, :], a["w0T"]), (w1T[:, :, :], a["w1T"]), (w2T[:, :, :], a["w2T"]),
                             (wfT[:, :, :], a["wfT"]), (tb[:, :], a["tb"]),
                             (bfb[:, :], a["bf"].partition_broadcast(P)),
                             (int2[:, :, :], a["interp2"])):
                sp.dma_start(dst, src).then_inc(misc_in, 16)
            for b in range(B):
                sp.dma_start(wfa[0:EMB, b, :], a["wfT"][:, 0, :]).then_inc(misc_in, 16)
            for k, (kind, src, *_) in enumerate(pieces):
                if before[k] is not None:
                    sp.wait_ge(lo_done, before[k] + 1)
                if kind == "wide":
                    sp.dma_start(stage[k], src).then_inc(part[k][0], 16)
                else:
                    sp.dma_start(stage[k][0:E2], src).then_inc(part[k][0], 16)
                    sp.dma_start(stage[k][E2:P], src).then_inc(part[k][0], 16)
                if k == 1:
                    sp.wait_ge(rows_done, 2)
                    for dst, _, row in bias_rows:
                        sp.dma_start(dst[1:2].bitcast(F32), row).then_inc(row_out, 16)
            for half in range(2):
                for c in range(8):
                    sp.wait_ge(tr_evac, order[("h", half, c)] + 1)
                    for r in range(2):
                        b = 2 * c + r
                        sp.dma_start(const["h"][b * N + half * P:b * N + (half + 1) * P, :],
                                     hout[:, (8 * half + c) % HB, r, :]).then_inc(h_out[(8 * half + c) % HB], 16)

        @block.scalar
        def _(act):
            for dst, src in ((keep["b1"][:, :], a["b1"]), (keep["ln_g1"][:, :], a["g1"].partition_broadcast(P)),
                             (keep["ln_b1"][:, :], a["be1"].partition_broadcast(P)),
                             (keep["ln_g3"][:, :], a["g3"].partition_broadcast(P)),
                             (keep["ln_b3"][:, :], a["be3"].partition_broadcast(P)),
                             (keep["ln_g4"][:, :], a["g4"].partition_broadcast(P)),
                             (keep["ln_b4"][:, :], a["be4"].partition_broadcast(P)),
                             (keep["ow_a"][:, :], a["owT"][0:P, :]), (keep["ow_c"][:, :], a["owT"][P:E, :]),
                             (keep["tri"][:, :, :], a["tri"].partition_broadcast(P))):
                act.dma_start(dst, src).then_inc(misc_in, 16)
            for half in range(2):
                if half:
                    act.wait_ge(tr_evac, order[("h", 0, 7)] + 1)
                for b in range(B):
                    act.dma_start(y0I[EMB:P, b * P:(b + 1) * P], a["interp1"][:, half * P:(half + 1) * P])\
                       .then_inc(interp_in, 16)
                if half == 0:
                    act.wait_ge(gathered2, 32)
                    act.dma_start(s2.rearrange("(m p) n -> p m n", p=P), g2[:, :, :]).then_inc(scratch_out, 16)
                    act.wait_ge(scratch_out, 16)
                    for b in range(B):
                        act.dma_start(
                            x2[(b % 8) * L2:(b % 8 + 1) * L2, b // 8, :].rearrange("t (j c) -> t j c", c=C2),
                            s2.rearrange("(t j) (b c) -> b t j c", j=GP, c=C2)[b]).then_inc(x2_in, 16)
                    act.wait_ge(gathered1, 8 * 16)
                    act.dma_start(s1.rearrange("(m p) n -> p m n", p=P), g1[:, :, :]).then_inc(scratch_out, 16)
                    act.wait_ge(scratch_out, 32)
                    for b in range(B):
                        act.dma_start(
                            x1[(b % 2) * L1:(b % 2 + 1) * L1, b // 2, :].rearrange("t (j c) -> t j c", c=C1),
                            s1.rearrange("(t j) (b c) -> b t j c", j=GP, c=C1)[b]).then_inc(x1_in, 16)
            for c in range(HB):
                act.wait_ge(h_out[c], 32 * ((16 - c + HB - 1) // HB))
            act.wait_ge(interp_in, 16 * 2 * B)
            act.wait_ge(misc_in, 16 * (10 + 7 + B))
            act.wait_ge(row_out, 16 * len(bias_rows))

        @block.gpsimd
        def _(pool):
            pool.wait_ge(idx_in, 48)
            for m in range(2):
                pool.indirect_dma_start(out=g2[:, m, :], out_offset=None, in_=a["x2r"],
                                        in_offset=bass.IndirectOffsetOnAxis(ap=idx2[:, m:m + 1], axis=0))\
                    .then_inc(gathered2, 16)
            pool.memset(ident[:, :], 0.0).then_inc(ident0, 1)
            pool.wait_ge(ident0, 1)
            pool.affine_select(out=ident[:, :], in_=ident[:, :], compare_op=ALU.not_equal, fill=1.0,
                               base=0, pattern=[[-1, P]], channel_multiplier=1).then_inc(ident_done, 1)
            for m in range(8):
                pool.indirect_dma_start(out=g1[:, m, :], out_offset=None, in_=a["x1r"],
                                        in_offset=bass.IndirectOffsetOnAxis(ap=idx1[:, m:m + 1], axis=0))\
                    .then_inc(gathered1, 16)
            for blk in range(2):
                for j in range(GP):
                    pool.indirect_dma_start(out=g0[:, blk, j, :], out_offset=None, in_=a["x0r"],
                                            in_offset=bass.IndirectOffsetOnAxis(ap=idx0[:, blk, j:j + 1], axis=0))\
                        .then_inc(gathered0[blk], 16)

        @block.tensor
        def _(pe):
            pe.wait_ge(ident_done, 1)
            pe.wait_ge(misc_in, 16 * (10 + 7 + B))

            def out(step):
                n = order[step]
                if n >= 8:
                    pe.wait_ge(tr_evac, n - 7)
                return bank[n % 8]

            pe.wait_ge(x2_in, 16 * B)
            for c in range(3):
                o = out(("x2T", c))
                for k in range(4):
                    q, r = (4 * c + k) // 2, k % 2
                    mm = pe.transpose(o[:, k * P:(k + 1) * P], x2[:, r, q * P:(q + 1) * P], ident[:, :])
                mm.then_inc(tr_done, 1)
            pe.wait_ge(tr_evac, 3)
            o = out(("y2", 0))
            for q in range(6):
                mm = pe.matmul(o[0:EMB, 0:B * L2], w2T[:, q, :], x2T[:, q, :], start=(q == 0), stop=(q == 5))
            mm.then_inc(tr_done, 1)
            pe.wait_ge(x1_in, 16 * B)
            for c in range(4):
                o = out(("x1T", c))
                for k in range(4):
                    q, r = c // 2, (c % 2) * 4 + k
                    mm = pe.transpose(o[0:96, k * P:(k + 1) * P], x1[:, r, q * 96:(q + 1) * 96], ident[:, :])
                mm.then_inc(tr_done, 1)
            pe.wait_ge(tr_evac, 8)
            for c in range(2):
                o = out(("y1", c))
                for q in range(2):
                    mm = pe.matmul(o[0:EMB, :], w1T[:, q, :], x1T[:, q, c * 512:(c + 1) * 512],
                                   start=(q == 0), stop=(q == 1))
                mm.then_inc(tr_done, 1)
            pe.wait_ge(tr_evac, 10)
            o = out(("a2", 0))
            for r in range(2):
                mm = pe.matmul(o[:, r * E:(r + 1) * E], y2T[:, r * P:(r + 1) * P], wfT[:, 2, :], start=True, stop=True)
            mm.then_inc(tr_done, 1)
            for c in range(8):
                o = out(("a1", c))
                for r in range(2):
                    b = 2 * c + r
                    mm = pe.matmul(o[EMB:P, r * E:(r + 1) * E], y1T[:, b * L1:(b + 1) * L1], wfT[:, 1, :],
                                   start=True, stop=True)
                mm.then_inc(tr_done, 1)
            for half in range(2):
                pe.wait_ge(gathered0[half], 16 * GP)
                for c in range(4):
                    o = out(("x0T", half, c))
                    for k in range(4):
                        b = 4 * c + k
                        mm = pe.transpose(o[0:GP * C0, k * P:(k + 1) * P], g0[:, half].rearrange("p j n -> p (j n)")[:, b::B],
                                          ident[:, :])
                    mm.then_inc(tr_done, 1)
                    pe.wait_ge(tr_evac, order[("x0T", half, c)] + 1)
                    o = out(("y0", half, c))
                    pe.matmul(o[0:EMB, :], w0T[:, :], x0T[:, c % 2, :], start=True, stop=True).then_inc(tr_done, 1)
                pe.wait_ge(interp_in, 16 * B * (half + 1))
                pe.wait_ge(tr_evac, order[("y0", half, 3)] + 1)
                for c in range(8):
                    o = out(("h", half, c))
                    for r in range(2):
                        b = 2 * c + r
                        g = 32 * (b % 8 // 2)
                        ob = o[:, r * E:(r + 1) * E]
                        pe.matmul(ob, y0I[:, b * P:(b + 1) * P], wfa[:, b, :], start=True, stop=False)
                        mm = pe.matmul(ob, int2[g:g + 32, b % 2, half * P:(half + 1) * P],
                                       a2[g:g + 32, b // 8, :], start=False, stop=True)
                        if r:
                            mm.then_inc(tr_done, 1)

        @block.vector
        def _(dve):
            dve.memset(keep["ones"][:, :].bitcast(F32), 1.0).then_inc(ones_done, 1)
            dve.wait_ge(rows_in, 16 * len(bias_rows))
            for dst, _, row in bias_rows:
                ins = dve.tensor_copy(dst[0:1], row)
            ins.then_inc(rows_done, 1)
            dve.wait_ge(rows_done, 1)
            for dst, _, row in bias_rows:
                ins = dve.tensor_tensor(row, row, dst[0:1].bitcast(F32), ALU.subtract)
            ins.then_inc(rows_done, 1)

            def split(k):
                kind, _, hi, lo, n = pieces[k]
                dve.wait_ge(*part[k])
                dve.tensor_copy(hi, stage[k]).then_inc(hi_done, 1)
                dve.wait_ge(hi_done, k + 1)
                if kind == "wide":
                    dve.tensor_tensor(lo, stage[k], hi.bitcast(F32), ALU.subtract).then_inc(lo_done, 1)
                else:
                    dve.tensor_tensor(hi[E2:P], stage[k][E2:P], hi[E2:P].bitcast(F32), ALU.subtract)\
                       .then_inc(lo_done, 1)

            def evac(step):
                n = order[step]
                src = bank[n % 8]
                dve.wait_ge(tr_done, n + 1)
                kind = step[0]
                if kind == "x2T":
                    c = step[1]
                    ins = dve.tensor_copy(x2T[:, 2 * c:2 * c + 2, :].rearrange("p q n -> p (q n)"), src[:, :])
                elif kind == "y2":
                    ins = dve.tensor_scalar(y2T[:, :], src[0:EMB, 0:B * L2], tb[:, 2:3], None, ALU.add)
                elif kind == "x1T":
                    c = step[1]
                    ins = dve.tensor_copy(x1T[:, c // 2, (c % 2) * 512:(c % 2 + 1) * 512], src[0:96, :])
                elif kind == "y1":
                    ins = dve.tensor_scalar(y1T[:, step[1] * 512:(step[1] + 1) * 512], src[0:EMB, :],
                                            tb[:, 1:2], None, ALU.add)
                elif kind == "a2":
                    ins = dve.tensor_copy(a2[:, :, :], src[:, 0:2 * E].rearrange("p (r n) -> p r n", r=2))
                elif kind == "a1":
                    c = step[1]
                    ins = dve.tensor_copy(wfa[EMB:P, 2 * c:2 * c + 2, :],
                                          src[EMB:P, 0:2 * E].rearrange("p (r n) -> p r n", r=2))
                elif kind == "x0T":
                    ins = dve.tensor_copy(x0T[:, step[2] % 2, :], src[0:GP * C0, :])
                elif kind == "y0":
                    ins = dve.tensor_scalar(y0I[0:EMB, step[2] * 512:(step[2] + 1) * 512], src[0:EMB, :],
                                            tb[:, 0:1], None, ALU.add)
                else:
                    half, c = step[1:]
                    n_h = 8 * half + c
                    if n_h >= HB:
                        dve.wait_ge(h_out[n_h % HB], 32 * (n_h // HB))
                    for r in range(2):
                        ins = dve.tensor_tensor(hout[:, n_h % HB, r, :], src[:, r * E:(r + 1) * E], bfb[:, :], ALU.add)
                ins.then_inc(tr_evac, 1)

            dve.wait_ge(misc_in, 16 * (10 + 7 + B))
            k = 0
            for step in steps[:19]:
                if k < len(pieces) and order[step] in (0, 4, 8, 11):
                    for _ in range(4):
                        split(k)
                        k += 1
                evac(step)
            while k < len(pieces):
                split(k)
                k += 1
            dve.wait_ge(row_out, 16 * len(bias_rows))
            for step in steps[19:]:
                evac(step)



NEG_AT = 10
LAG = 3
BESIDE = ([("start", 0, 8), ("parts", 0, 2), ("heads0", 0, 1), ("ready", 0, 1)] + [("max0", 0, 0)] * 4
          + [("heads1", 0, 1), ("next", 0, 1), ("both", 0, 0), ("mid", 0, 0), ("exp1", 0, 1), ("end", 0, 3)]
          + [("start", 1, 14), ("parts", 1, 2), ("heads0", 1, 2), ("ready", 1, 2)] + [("max0", 1, 2)] * 4
          + [("heads1", 1, 4), ("next", 1, 2), ("both", 1, 2), ("mid", 1, 2), ("exp1", 1, 1), ("end", 1, 2),
             ("proj", 1, 3), ("over", 1, 99)])


def ffn_steps():
    def tiles(c0, c1):
        out = [("up", c0)]
        for c in range(c0 + 1, c1):
            out += [("up", c), ("down", c - 1)]
        return out + [("down", c1 - 1)]

    return ([("split", 2)] + tiles(0, MT) + [("sum", 0), ("norm", 4), ("split", 3), ("gate", 0)] + tiles(MT, MT * NMLP)
            + [("last", 0)])


def place_steps():
    steps, at_point, seen = ffn_steps(), {}, {}
    for phase, layer, count in BESIDE:
        n = seen[phase, layer] = seen.get((phase, layer), -1) + 1
        at_point[phase, layer, n], steps = steps[:count], steps[count:]
    assert not steps
    return at_point


def tower(nc, keep, const, out):
    with ExitStack() as ctx:
        sb = lambda name, shape, dt=F32: ctx.enter_context(nc.sbuf_tensor(name, shape, dt))
        sem = lambda name: ctx.enter_context(nc.semaphore(name))
        pb = lambda name: ctx.enter_context(nc.psum_tensor(name, [P, 512], F32))

        NR, NPROB = 3, 4
        ring_bank = [pb(f"ring{k}") for k in range(NR)]
        ctx_bank = pb("ctx_bank")
        hid_bank = [pb("hid_bank0"), pb("hid_bank1")]
        mlp_bank = [pb("mlp_bank0"), pb("mlp_bank1")]
        ident = keep["ident"]

        h = sb("h", [P, NBLK, E])
        u = sb("u", [P, NBLK, E])
        y = sb("y", [P, NBLK, E])
        x = sb("x", [P, NBLK, E])
        xparts = [(sb(f"xh{k}", [P, T], F32R), sb(f"xl{k}", [P, T], F32R), sb(f"xch{k}", [P, T], F32R),
                   sb(f"xcl{k}", [E2, T], F32R)) for k in range(2)]
        qs, ks = sb("qs", [P, 2, H, DS]), sb("ks", [P, 2, H, DS])
        kT = [sb(f"kT{b}", [P, HP, N], F32R) for b in range(2)]
        qT = [sb(f"qT{b}", [P, HP, N], F32R) for b in range(2)]
        v = sb("v", [P, 2, 2, H, 2 * D])
        prob = sb("prob", [P, NPROB, 2, N])
        cT = sb("cT", [P, 3 * N])
        mx = sb("mx", [P, 2, 2, HP])
        ms = sb("ms", [P, 2, 2, 2, HP], F32R)
        msT = keep["bias"][96:96 + 4 * HP, 0:N]
        rsum = sb("rsum", [P, 2, H])
        st, mv = sb("st", [P, NBLK, 6]), sb("mv", [P, NBLK, 2])
        spare = prob[:, :, :, :].rearrange("p a b n -> p (a b n)")
        fresh = spare[:, 0:NBLK * E].rearrange("p (c e) -> p c e", c=NBLK)
        ctxT = [spare[:, 2 * T:3 * T], spare[:, 3 * T:4 * T]]
        ve, yn, hv, tn = (sb(name, [P, NBLK]) for name in ("ve", "yn", "hv", "tn"))
        sh = sb("sh", [P, NBLK], I32)
        lg, ex = sb("lg", [P, NBLK, NEXP]), sb("ex", [P, NBLK, NEXP])
        rank, comb = sb("rank", [P, NBLK, NEXP]), sb("comb", [P, NBLK, NEXP])
        m1, s1 = sb("m1", [P, NBLK]), sb("s1", [P, NBLK])
        gel_xm = sb("gel_xm", [P, NBLK * E])
        gel = gel_xm[:, 0:T]
        xm = gel_xm[:, :].rearrange("p (c e) -> p c e", c=NBLK)
        gt4, eq4 = (gel_xm[:, T + k * NBLK * NEXP ** 2:T + (k + 1) * NBLK * NEXP ** 2]
                    .rearrange("p (c j e) -> p c j e", c=NBLK, j=NEXP) for k in range(2))
        gh, gl = sb("gh", [P, 2, T], F32R), sb("gl", [P, 2, T], F32R)

        ring = Ring(ring_products(), [sem(f"ring_full{k}") for k in range(NR)],
                    [sem(f"ring_read{k}") for k in range(NR)])
        hid = Ring(hid_products(), [sem(f"hid_full{k}") for k in range(2)], [sem(f"hid_read{k}") for k in range(2)])
        u_in, h_in = sem("u_in"), sem("h_in")
        stored = sem("stored")
        neg_in = sem("neg_in")
        zeroed = sem("zeroed")
        passed = sem("passed")
        CHAIN = 6 + 3 * NEWTON
        PER = dict(ln_chain=CHAIN * 4, ln4_chain=CHAIN, ln_affine=2, ln4_affine=1, ln_out=4, ln4_out=1, y_sum=NBLK, h_sum=1,
                   res=1, hi_copy=4, fhi_copy=4, qk_hi=8, neg_hi=4, neg_done=4, pv_done=24,
                   cbank_read=12, rs_done=8, gl_done=MT * NMLP,
                   down_done=MT * NMLP, acc_read=NMLP, gate_chain=12, gate_exp=1)
        S = {name: sem(name) for name in PER}
        points = place_steps()
        block = ctx.enter_context(nc.Block())

        def at(i, name, n):
            return S[name], ev(i, PER[name], n)

        def credit(eng, *names):
            for name in names:
                eng.sem_inc(S[name], PER[name])

        def plan_of(name):
            return (ring, ring_bank) if name in ring.slot else (hid, hid_bank)

        def slot(name):
            plan, banks = plan_of(name)
            return banks[plan.slot[name]]

        def read_sem(name):
            plan, _ = plan_of(name)
            return plan.read_sem[plan.slot[name]]

        def full_sem(name):
            plan, _ = plan_of(name)
            return plan.full_sem[plan.slot[name]]

        def full(i, name):
            return plan_of(name)[0].full(i, name)

        def read(i, name):
            return plan_of(name)[0].read(i, name)

        def room(i, name):
            return plan_of(name)[0].room(i, name)

        def pipeline(eng, attention, ffn):
            attention(0, lambda point: None)
            with eng.Fori(1, NIT) as i:
                def beside(point):
                    for step in points[point]:
                        ffn(i - 1, *step)
                attention(i, beside)
            for step in ffn_steps():
                ffn(NIT - 1, *step)

        def beside_all(beside, layer, *phases):
            for point in points:
                if point[0] in phases and point[1] == layer:
                    beside(point)

        @block.sync
        def _(sp):
            sp.sem_inc(stored, 16)
            sp.sem_inc(neg_in, 4 * 64)
            hd = const["h"].rearrange("(i c p) e -> i p c e", p=P, c=NBLK)
            od = out.rearrange("b n e -> (b n) e").rearrange("(i c p) e -> i p c e", p=P, c=NBLK)

            def attention(i, beside):
                src = hd[i]
                sp.wait_ge(*at(i - 1, "pv_done", PER["pv_done"] - 1))
                sp.dma_start(fresh, src).then_inc(u_in, 16)
                if isinstance(i, int):
                    sp.dma_start(h[:, :, :], src).then_inc(h_in, 16)
                for a in range(2):
                    beside_all(beside, a, "start", "parts", "heads0", "ready", "max0", "heads1", "next")
                    for b in range(2):
                        sp.wait_ge(*ring.read(i, ("negmax", a, b)))
                        for p in range(2):
                            for r in range(2):
                                row = 64 * p + 3 * D + r
                                sp.dma_start(qT[b][row:row + 1, :, :].bitcast(F32),
                                             msT[(2 * p + r) * HP:(2 * p + r + 1) * HP, :].bitcast(F32)).then_inc(neg_in, 16)
                        if b == 0:
                            beside(("both", a, 0))
                    beside_all(beside, a, "mid", "exp1", "end", "proj", "over")

            def ffn(i, kind, c):
                if kind == "split" and c == 3 and not isinstance(i, int):
                    src = hd[i + 1]
                    sp.wait_ge(*at(i, "res", 0))
                    sp.dma_start(h[:, :, :], src).then_inc(h_in, 16)
                if kind == "last":
                    dst = od[i]
                    sp.wait_ge(*at(i, "acc_read", NMLP - 1))
                    sp.dma_start(dst, x[:, :, :]).then_inc(stored, 16)

            pipeline(sp, attention, ffn)
            sp.wait_ge(stored, 16 * (NIT + 1))

        @block.gpsimd
        def _(pool):
            pool.memset(v[:, :, :, :, :], 0.0).then_inc(zeroed, 1)
            pool.memset(qs[:, :, :, :], 0.0).then_inc(zeroed, 1)
            pool.memset(ks[:, :, :, :], 0.0).then_inc(zeroed, 1)
            pool.wait_ge(zeroed, 3)
            pool.memset(v[:, :, :, :, D:D + 1], 1.0).then_inc(zeroed, 1)
            pool.memset(ks[:, :, :, 3 * D:3 * D + 2], 1.0).then_inc(zeroed, 1)
            credit(pool, "y_sum", "res", "gl_done")

            def attention(i, beside):
                for a in range(2):
                    beside_all(beside, a, "start", "parts", "heads0", "ready", "max0", "heads1", "next", "both",
                               "mid")
                    if a == 1:
                        beside_all(beside, a, "exp1", "end", "proj", "over")
                        break
                    for b in range(2):
                        if b == 1:
                            beside_all(beside, a, "exp1")
                        for half in range(2):
                            pool.wait_ge(*ring.read(i, ("ctx", 0, b, half)))
                            pool.tensor_tensor(y[:, 2 * b + half], y[:, 2 * b + half], u[:, 2 * b + half], ALU.add)\
                                .then_inc(S["y_sum"], 1)
                    beside_all(beside, a, "end")

            def ffn(i, kind, c):
                if kind == "up":
                    pool.wait_ge(*hid.read(i, ("up", c)))
                    pool.tensor_tensor(gl[:, c % 2], gel, gh[:, c % 2].bitcast(F32), ALU.subtract)\
                        .then_inc(S["gl_done"], 1)
                if kind == "split" and c == 3:
                    pool.wait_ge(*at(i, "ln4_out", 0))
                    pool.tensor_tensor(x[:, :, :], x[:, :, :], h[:, :, :], ALU.add).then_inc(S["res"], 1)

            pipeline(pool, attention, ffn)

        @block.scalar
        def _(act):
            act.wait_ge(zeroed, 5)
            credit(act, "hi_copy", "fhi_copy", "qk_hi", "cbank_read", "gate_exp")

            def split_hi(i, s):
                xh, _, xch, _ = xparts[s // 2]
                done = S["fhi_copy" if s >= 2 else "hi_copy"]
                name = ("split_a", s)
                act.wait_ge(*full(i, name))
                act.copy(xh[:, :], slot(name)[:, :]).then_inc(done, 1)
                name = ("split_c", s)
                act.wait_ge(*full(i, name))
                act.copy(xch[0:E2, :], slot(name)[0:E2, :])
                act.copy(xch[E2:P, :], slot(name)[0:E2, :]).then_inc(done, 1)

            def prepare(i, a, b, beside):
                for half in range(2):
                    name = ("qk", a, b, half)
                    act.wait_ge(*ring.full(i, name))
                    src = slot(name)[:, 0:2 * E].rearrange("p (x h d) -> p x h d", x=2, h=H)
                    for dst, which, off in ((qs, 0, 0), (qs, 0, D), (ks, 1, 0), (ks, 1, 2 * D)):
                        ins = act.copy(dst[:, half, :, off:off + D].bitcast(F32R), src[:, which])
                    ins.then_inc(S["qk_hi"], 1)
                name = ("v", a, b)
                act.wait_ge(*ring.full(i, name))
                act.copy(v[:, b, :, :, 0:D], slot(name)[:, 0:2 * E].rearrange("p (x h d) -> p x h d", x=2, h=H))\
                   .then_inc(read_sem(name), 1)
                beside((f"heads{b}", a, 0))
                for g in range(3):
                    name = ("k", a, b, g)
                    act.wait_ge(*ring.full(i, name))
                    act.copy(kT[b][:, 2 * g:2 * g + 2, :], slot(name)[:, :].rearrange("p (g n) -> p g n", g=2))\
                       .then_inc(read_sem(name), 1)

            def negmax(i, a, b):
                name = ("negmax", a, b)
                act.wait_ge(*ring.full(i, name))
                act.wait_ge(neg_in, 64 * (4 * (i + 1) + 2 * a + b))
                act.copy(msT, slot(name)[0:4 * HP, 0:N]).then_inc(read_sem(name), 1)

            def exp(i, a, b, n):
                name = ("score", a, b, n)
                act.wait_ge(*ring.full(i, name))
                act.wait_ge(*at(i, "pv_done", 6 * (2 * a + b) + n // 2 - NPROB // 2))
                act.activation(prob[:, n % NPROB], slot(name)[:, :].rearrange("p (g n) -> p g n", g=2), ACT.Exp,
                               scale=float(D) ** -0.5).then_inc(read_sem(name), 1)

            def context(i, a, b, g):
                n = 3 * (2 * a + b) + g
                act.wait_ge(*at(i, "pv_done", 2 * n + 1))
                act.copy(cT[:, g * N:(g + 1) * N], ctx_bank[:, 0:N])\
                   .then_inc(S["cbank_read"], 1)

            def ffn(i, kind, c):
                if kind == "split":
                    split_hi(i, c)
                if kind == "up":
                    name, e, m = ("up", c), c // MT, c % MT
                    act.wait_ge(*hid.full(i, name))
                    act.wait_ge(*at(i, "down_done", c - 2))
                    bias = keep["b1"][:, e * MT + m:e * MT + m + 1]
                    act.activation(gh[:, c % 2], slot(name)[:, :], ACT.Gelu, bias=bias)
                    act.wait_ge(*at(i, "gl_done", c - 1))
                    act.activation(gel, slot(name)[:, :], ACT.Gelu, bias=bias).then_inc(read_sem(name), 1)
                if kind == "gate":
                    act.wait_ge(*at(i, "gate_chain", 1))
                    act.activation(ex[:, :, :], ex[:, :, :], ACT.Exp).then_inc(S["gate_exp"], 1)

            def attention(i, beside):
                for a in range(2):
                    beside(("start", a, 0))
                    split_hi(i, a)
                    beside(("parts", a, 0))
                    prepare(i, a, 0, beside)
                    beside_all(beside, a, "ready", "max0")
                    prepare(i, a, 1, beside)
                    beside_all(beside, a, "next")
                    negmax(i, a, 0)
                    beside(("both", a, 0))
                    for b in range(2):
                        for n in range(12):
                            exp(i, a, b, n)
                            if n in (5, 9):
                                context(i, a, b, n // 4 - 1)
                            if b == 0 and n == NEG_AT:
                                negmax(i, a, 1)
                        context(i, a, b, 2)
                    beside_all(beside, a, "mid", "exp1", "end")
                for k, rows in enumerate((P, E2)):
                    act.wait_ge(*ring.full(i, ("ctxT", k)))
                    act.copy(ctxT[k][0:rows, :], slot(("ctxT", k))[0:rows, :])\
                       .then_inc(read_sem(("ctxT", k)), 1)
                beside(("proj", 1, 0))
                beside(("over", 1, 0))

            pipeline(act, attention, ffn)

        @block.vector
        def _(dve):
            credit(dve, "ln_chain", "ln4_chain", "ln_affine", "ln4_affine", "ln_out", "ln4_out", "h_sum", "neg_hi", "neg_done",
                   "rs_done", "acc_read", "gate_chain")
            for plan in (ring, hid):
                for s, n in zip(plan.read_sem, plan.per):
                    dve.sem_inc(s, n)

            def norm(i, k, src, dst, gamma=None, beta=None, early=0):
                name, k0 = ("ln4_chain", 0) if k == 4 else ("ln_chain", k)
                done, step = S[name], iter(range(CHAIN * k0, CHAIN * (k0 + 1)))

                def after(ins):
                    ins.then_inc(done, 1)
                    dve.wait_ge(*at(i, name, next(step)))

                for blk in range(early, NBLK):
                    if k == 1:
                        dve.wait_ge(*at(i, "y_sum", blk))
                    ins = dve.bn_stats(st[:, blk, :], src[:, blk, :])
                after(ins)
                dve.sem_inc(passed, 1)
                for blk in range(NBLK):
                    ins = dve.bn_aggr(mv[:, blk, :], st[:, blk, :])
                after(ins)
                after(dve.tensor_scalar(ve[:, :], mv[:, :, 1], EPS, None, ALU.add))
                after(dve.tensor_scalar(sh[:, :], ve[:, :].bitcast(I32), 1, None, ALU.logical_shift_right))
                after(dve.tensor_scalar(hv[:, :], ve[:, :], -0.5, None, ALU.mult))
                after(dve.tensor_scalar(yn[:, :].bitcast(I32), sh[:, :], -1.0, MAGIC, ALU.mult, ALU.add))
                for _ in range(NEWTON):
                    after(dve.tensor_tensor(tn[:, :], yn[:, :], yn[:, :], ALU.mult))
                    after(dve.tensor_tensor(tn[:, :], tn[:, :], hv[:, :], ALU.mult))
                    after(dve.scalar_tensor_tensor(out=yn[:, :], in0=tn[:, :], scalar=1.5, in1=yn[:, :],
                                                   op0=ALU.add, op1=ALU.mult))
                if gamma is None:
                    for blk in range(NBLK):
                        ins = dve.tensor_scalar(dst[:, blk], src[:, blk], mv[:, blk, 0:1], yn[:, blk:blk + 1],
                                                ALU.subtract, ALU.mult)
                else:
                    for blk in range(NBLK):
                        ins = dve.scalar_tensor_tensor(out=dst[:, blk], in0=src[:, blk], scalar=mv[:, blk, 0:1],
                                                       in1=gamma[:, :], op0=ALU.subtract, op1=ALU.mult)
                    affine = "ln4_affine" if k == 4 else "ln_affine"
                    ins.then_inc(S[affine], 1)
                    dve.wait_ge(*at(i, affine, k0 // 2))
                    for blk in range(NBLK):
                        ins = dve.scalar_tensor_tensor(out=dst[:, blk], in0=dst[:, blk], scalar=yn[:, blk:blk + 1],
                                                       in1=beta[:, :], op0=ALU.mult, op1=ALU.add)
                name = "ln4_out" if k == 4 else "ln_out"
                ins.then_inc(S[name], 1)
                dve.wait_ge(*at(i, name, k0))

            def split_lo(i, s):
                xh, xl, xch, xcl = xparts[s // 2]
                for k, (name, hi, lo, rows) in enumerate(((("split_a", s), xh, xl, P), (("split_c", s), xch, xcl, E2))):
                    dve.wait_ge(*at(i, "fhi_copy" if s >= 2 else "hi_copy", 2 * (s % 2) + k))
                    dve.tensor_tensor(lo[:, :], slot(name)[0:rows, :], hi[0:rows, :].bitcast(F32), ALU.subtract)\
                       .then_inc(read_sem(name), 1)

            def prepare(i, a, b, beside):
                for half in range(2):
                    name = ("qk", a, b, half)
                    dve.wait_ge(*at(i, "qk_hi", 2 * (2 * a + b) + half))
                    src = slot(name)[:, 0:2 * E].rearrange("p (x h d) -> p x h d", x=2, h=H)
                    dve.tensor_tensor(qs[:, half, :, 2 * D:3 * D].bitcast(F32R), src[:, 0], qs[:, half, :, 0:D],
                                      ALU.subtract)
                    dve.tensor_tensor(ks[:, half, :, D:2 * D].bitcast(F32R), src[:, 1], ks[:, half, :, 0:D],
                                      ALU.subtract).then_inc(read_sem(name), 1)
                beside((f"heads{b}", a, 0))
                for g in range(3):
                    name = ("q", a, b, g)
                    dve.wait_ge(*ring.full(i, name))
                    dve.tensor_copy(qT[b][:, 2 * g:2 * g + 2, :], slot(name)[:, :].rearrange("p (g n) -> p g n", g=2))\
                       .then_inc(read_sem(name), 1)

            def maximum(i, a, b, n):
                name = ("max", a, b, n)
                dve.wait_ge(*ring.full(i, name))
                dve.tensor_reduce(mx[:, n // HP, n % 2, n % HP // 2 * 2:n % HP // 2 * 2 + 2],
                                  slot(name)[:, :].rearrange("p (g n) -> p g n", g=2),
                                  AX.X, ALU.max).then_inc(read_sem(name), 1)

            def negate(i, a, b):
                for n in (9, 10, 11):
                    dve.wait_ge(*ring.read(i, ("max", a, b, n)))
                dve.tensor_scalar(ms[:, :, :, 0, :], mx[:, :, :, :], -1.0, None, ALU.mult).then_inc(S["neg_hi"], 1)
                dve.wait_ge(*at(i, "neg_hi", 2 * a + b))
                for half in range(2):
                    ins = dve.scalar_tensor_tensor(out=ms[:, half, :, 1, :], in0=mx[:, half], scalar=-1.0,
                                                   in1=ms[:, half, :, 0, :].bitcast(F32), op0=ALU.mult,
                                                   op1=ALU.subtract)
                ins.then_inc(S["neg_done"], 1)

            def context(i, a, b):
                for half in range(2):
                    name = ("ctx", a, b, half)
                    dve.wait_ge(*ring.full(i, name))
                    src = slot(name)[:, 0:3 * P].rearrange("p (h d) -> p h d", d=2 * D)
                    dve.reciprocal(rsum[:, half, :], src[:, :, D]).then_inc(S["rs_done"], 1)
                    dve.wait_ge(*at(i, "rs_done", 2 * (2 * a + b) + half))
                    dve.tensor_tensor(y[:, 2 * b + half, :].rearrange("p (h d) -> p h d", d=D), src[:, :, 0:D],
                                      rsum[:, half, :].unsqueeze(2).to_broadcast([P, H, D]), ALU.mult)\
                       .then_inc(read_sem(name), 1)

            def gate(i):
                chain, step = S["gate_chain"], iter(range(12))

                def after(ins):
                    ins.then_inc(chain, 1)
                    dve.wait_ge(*at(i, "gate_chain", next(step)))

                dve.wait_ge(*full(i, ("gate",)))
                dve.tensor_copy(lg[:, :, :], slot(("gate",))[:, 0:NBLK * NEXP].rearrange("p (c e) -> p c e", c=NBLK))\
                   .then_inc(read_sem(("gate",)), 1)
                dve.wait_ge(*read(i, ("gate",)))
                l_j = lg[:, :, :].unsqueeze(2).to_broadcast([P, NBLK, NEXP, NEXP])
                l_e = lg[:, :, :].unsqueeze(3).to_broadcast([P, NBLK, NEXP, NEXP])
                after(dve.tensor_reduce(m1[:, :], lg[:, :, :], AX.X, ALU.max))
                after(dve.tensor_tensor(ex[:, :, :], lg[:, :, :],
                                        m1[:, :].unsqueeze(2).to_broadcast([P, NBLK, NEXP]), ALU.subtract))
                after(dve.tensor_tensor(gt4[:, :, :, :], l_j, l_e, ALU.is_gt))
                after(dve.tensor_tensor(eq4[:, :, :, :], l_j, l_e, ALU.is_equal))
                after(dve.tensor_tensor(eq4[:, :, :, :], eq4[:, :, :, :],
                                        keep["tri"][:, :, :].unsqueeze(1).to_broadcast([P, NBLK, NEXP, NEXP]),
                                        ALU.mult))
                after(dve.tensor_tensor(gt4[:, :, :, :], gt4[:, :, :, :], eq4[:, :, :, :], ALU.add))
                after(dve.tensor_reduce(rank[:, :, :], gt4[:, :, :, :], AX.X, ALU.add))
                after(dve.tensor_scalar(rank[:, :, :], rank[:, :, :], 1.5, None, ALU.is_lt))
                dve.wait_ge(*at(i, "gate_exp", 0))
                after(dve.tensor_tensor(ex[:, :, :], ex[:, :, :], rank[:, :, :], ALU.mult))
                after(dve.tensor_reduce(s1[:, :], ex[:, :, :], AX.X, ALU.add))
                after(dve.reciprocal(s1[:, :], s1[:, :]))
                after(dve.tensor_tensor(comb[:, :, :], ex[:, :, :],
                                        s1[:, :].unsqueeze(2).to_broadcast([P, NBLK, NEXP]), ALU.mult))

            def expert_sum(i, e):
                if e == 1:
                    dve.wait_ge(*at(i, "res", 0))
                dve.wait_ge(*at(i, "down_done", MT * (e + 1) - 1))
                dve.wait_ge(*at(i, "acc_read", e - 1))
                for blk in range(NBLK):
                    src = mlp_bank[blk // 2][:, (blk % 2) * E:(blk % 2 + 1) * E]
                    ins = dve.scalar_tensor_tensor(out=x[:, blk], in0=src, scalar=comb[:, blk, e - 1:e],
                                                   in1=x[:, blk], op0=ALU.mult, op1=ALU.add)
                ins.then_inc(S["acc_read"], 1)

            def ffn(i, kind, c):
                if kind == "split":
                    split_lo(i, c)
                if kind == "sum":
                    dve.wait_ge(stored, 16 * i + 16)
                    dve.wait_ge(*at(i, "down_done", MT - 1))
                    for j in range(2):
                        ins = dve.tensor_tensor(x[:, 2 * j:2 * j + 2],
                                                mlp_bank[j][:, 0:2 * E].rearrange("p (c e) -> p c e", c=2),
                                                y[:, 2 * j:2 * j + 2], ALU.add)
                    ins.then_inc(S["acc_read"], 1)
                if kind == "norm":
                    dve.wait_ge(*at(i, "acc_read", 0))
                    norm(i, 4, x, xm, keep["ln_g4"], keep["ln_b4"])
                if kind == "gate":
                    gate(i)
                if kind == "up" and c % MT == 1 and c > 2 * MT:
                    expert_sum(i, c // MT - 1)
                if kind == "last":
                    expert_sum(i, NEXP)

            def attention(i, beside):
                for a in range(2):
                    if a == 0:
                        beside(("start", 0, 0))
                        dve.wait_ge(u_in, 16 * i + 16)
                        norm(i, 0, fresh, u)
                    split_lo(i, a)
                    beside(("parts", a, 0))
                    prepare(i, a, 0, beside)
                    beside(("ready", a, 0))
                    for n in range(12):
                        maximum(i, a, 0, n)
                        if n % 3 == 2:
                            beside(("max0", a, n // 3))
                    negate(i, a, 0)
                    prepare(i, a, 1, beside)
                    beside(("next", a, 0))
                    for n in range(12):
                        maximum(i, a, 1, n)
                        if n == LAG:
                            beside(("both", a, 0))
                    negate(i, a, 1)
                    beside(("mid", a, 0))
                    context(i, a, 0)
                    beside(("exp1", a, 0))
                    if a == 0:
                        for blk in range(2):
                            dve.wait_ge(*at(i, "y_sum", blk))
                            dve.bn_stats(st[:, blk, :], y[:, blk, :])
                    context(i, a, 1)
                    beside(("end", a, 0))
                    if a == 0:
                        norm(i, 1, y, y, keep["ln_g1"], keep["ln_b1"], early=2)
                        dve.wait_ge(h_in, 16 * i + 16)
                        dve.tensor_tensor(h[:, :, :], h[:, :, :], y[:, :, :], ALU.add).then_inc(S["h_sum"], 1)
                        dve.wait_ge(*at(i, "h_sum", 0))
                        norm(i, 2, h, u)
                        beside(("start", 1, 0))
                        norm(i, 3, u, y, keep["ln_g3"], keep["ln_b3"])
                beside(("proj", 1, 0))
                for j in range(2):
                    name = ("proj", j)
                    dve.wait_ge(*ring.full(i, name))
                    dve.tensor_tensor(y[:, 2 * j:2 * j + 2], slot(name)[:, 0:2 * E].rearrange("p (c e) -> p c e", c=2),
                                      u[:, 2 * j:2 * j + 2], ALU.add).then_inc(read_sem(name), 1)
                beside(("over", 1, 0))

            pipeline(dve, attention, ffn)

        @block.tensor
        def _(pe):
            credit(pe, "pv_done", "down_done")
            for plan in (ring, hid):
                for s, n in zip(plan.full_sem, plan.per):
                    pe.sem_inc(s, n)

            def split(i, s, src):
                pe.wait_ge(*room(i, ("split_c", s)))
                name = ("split_a", s)
                pe.wait_ge(*room(i, name))
                for blk in range(NBLK):
                    mm = pe.transpose(slot(name)[:, blk * P:(blk + 1) * P], src[:, blk, 0:P], ident[:, :])
                mm.then_inc(full_sem(name), 1)
                name = ("split_c", s)
                for blk in range(NBLK):
                    mm = pe.transpose(slot(name)[0:E2, blk * P:(blk + 1) * P], src[:, blk, P:E], ident[:, :])
                mm.then_inc(full_sem(name), 1)

            def bias_of(q, c0, c1):
                return keep["ones"][q:q + 2, :], keep["bias"][q:q + 2, c0:c1]

            def tokens_by(o, parts, blk, wh, wl, wc, bias):
                xh, xl, xch, xcl = parts
                t = slice(blk * P, (blk + 1) * P)
                pe.matmul(o, *bias, start=True, stop=False)
                pe.matmul(o, xh[:, t], wh, start=False, stop=False)
                pe.matmul(o, xh[:, t], wl, start=False, stop=False)
                pe.matmul(o, xl[:, t], wh, start=False, stop=False)
                pe.matmul(o, xch[:, t], wc, start=False, stop=False)
                return pe.matmul(o, xcl[:, t], wc[0:E2], start=False, stop=True)

            def prepare(i, a, b, beside):
                wh, wl, wc = (keep[k][:, a] for k in ("wq_h", "wq_l", "wq_c"))
                for half in range(2):
                    name = ("qk", a, b, half)
                    pe.wait_ge(*ring.room(i, name))
                    tokens_by(slot(name)[:, 0:2 * E], xparts[0], 2 * b + half, wh[:, 0:2 * E], wl[:, 0:2 * E],
                              wc[:, 0:2 * E], bias_of(BIAS_AT[a], 0, 2 * E)).then_inc(full_sem(name), 1)
                name = ("v", a, b)
                pe.wait_ge(*ring.room(i, name))
                for half in range(2):
                    mm = tokens_by(slot(name)[:, half * E:(half + 1) * E], xparts[0], 2 * b + half, wh[:, 2 * E:],
                                   wl[:, 2 * E:], wc[:, 2 * E:], bias_of(BIAS_AT[a], 2 * E, 3 * E))
                mm.then_inc(full_sem(name), 1)
                beside((f"heads{b}", a, 0))
                for half in range(2):
                    pe.wait_ge(*ring.read(i, ("qk", a, b, half)))
                for x_, src in (("k", ks), ("q", qs)):
                    for g in range(3):
                        name = (x_, a, b, g)
                        pe.wait_ge(*ring.room(i, name))
                        for k in range(4):
                            hp, half = 2 * g + k // 2, k % 2
                            mm = pe.transpose(slot(name)[:, k * P:(k + 1) * P],
                                              src[:, half, 2 * hp:2 * hp + 2, :].rearrange("p h d -> p (h d)"),
                                              ident[:, :])
                        mm.then_inc(full_sem(name), 1)

            def maximum(i, a, b, n):
                name, half, g, p = ("max", a, b, n), n // HP, n % HP // 2, n % 2
                r = slice(64 * p, 64 * p + 3 * D)
                if n == 0:
                    for k in range(3):
                        pe.wait_ge(*ring.read(i, ("q", a, b, k)))
                pe.wait_ge(*ring.room(i, name))
                for k in range(2):
                    mm = pe.matmul(slot(name)[:, k * N:(k + 1) * N], qT[b][r, 2 * g + k, half * P:(half + 1) * P],
                                   kT[b][r, 2 * g + k, :], start=True, stop=True)
                mm.then_inc(full_sem(name), 1)

            def negmax(i, a, b):
                name = ("negmax", a, b)
                pe.wait_ge(*at(i, "neg_done", 2 * a + b))
                pe.wait_ge(*ring.room(i, name))
                for half in range(2):
                    mm = pe.transpose(slot(name)[0:4 * HP, half * P:(half + 1) * P],
                                      ms[:, half].rearrange("p a r h -> p (a r h)").bitcast(F32), ident[:, :])
                mm.then_inc(full_sem(name), 1)

            def score(i, a, b, n):
                name, g, kb, p = ("score", a, b, n), n // 4, n // 2 % 2, n % 2
                r = slice(64 * p, 64 * p + 3 * D + 2)
                if n == 0:
                    pe.wait_ge(neg_in, 64 * (4 * (i + 1) + 2 * a + b + 1))
                pe.wait_ge(*ring.room(i, name))
                for k in range(2):
                    mm = pe.matmul(slot(name)[:, k * N:(k + 1) * N], kT[b][r, 2 * g + k, kb * P:(kb + 1) * P],
                                   qT[b][r, 2 * g + k, :], start=True, stop=True)
                mm.then_inc(full_sem(name), 1)

            def pv(i, a, b, w):
                g, kb = w // 2, w % 2
                n = 3 * (2 * a + b) + g
                if w == 0:
                    pe.wait_ge(*ring.read(i, ("v", a, b)))
                if kb == 0:
                    pe.wait_ge(*at(i, "cbank_read", n - 1))
                for k in range(2):
                    pe.wait_ge(*ring.read(i, ("score", a, b, 2 * w + k)))
                for j in range(4):
                    mm = pe.matmul(ctx_bank[32 * j:32 * j + 32, 0:N],
                                   v[:, b, kb, 4 * g + j, :], prob[:, (2 * w + j % 2) % NPROB, j // 2, :],
                                   start=(kb == 0), stop=(kb == 1))
                mm.then_inc(S["pv_done"], 1)

            def context(i, a, b):
                pe.wait_ge(*at(i, "cbank_read", 3 * (2 * a + b) + 2))
                for half in range(2):
                    name = ("ctx", a, b, half)
                    pe.wait_ge(*ring.room(i, name))
                    for g in range(3):
                        mm = pe.transpose(slot(name)[:, g * P:(g + 1) * P],
                                          cT[:, g * N + half * P:g * N + (half + 1) * P], ident[:, :])
                    mm.then_inc(full_sem(name), 1)

            def up(i, c):
                name, e, m = ("up", c), c // MT, c % MT
                xh, xl, xch, xcl = xparts[1]
                w = slice(m * P, (m + 1) * P)
                if c == 0:
                    pe.wait_ge(*read(i, ("split_c", 2)))
                pe.wait_ge(*room(i, name))
                o = slot(name)[:, :]
                wh, wl, wc = keep["w1_h"][:, e, w], keep["w1_l"][:, e, w], keep["w1_c"][:, e, w]
                pe.matmul(o, wh, xh[:, :], start=True, stop=False)
                pe.matmul(o, wh, xl[:, :], start=False, stop=False)
                pe.matmul(o, wl, xh[:, :], start=False, stop=False)
                pe.matmul(o, wc, xch[:, :], start=False, stop=False)
                pe.matmul(o, wc[0:E2], xcl[:, :], start=False, stop=True).then_inc(full_sem(name), 1)

            def down(i, c):
                e, m = c // MT, c % MT
                o = [mlp_bank[blk // 2][:, (blk % 2) * E:(blk % 2 + 1) * E] for blk in range(NBLK)]
                if m == 0:
                    pe.wait_ge(*at(i, "acc_read", e - 1))
                    for blk in range(NBLK):
                        pe.matmul(o[blk], *bias_of(BIAS_AT[2], e * E, (e + 1) * E), start=(blk % 2 == 0), stop=False,
                                  skip_group_check=True)
                pe.wait_ge(*at(i, "gl_done", c))
                wh, wl = keep["w2_h"][:, e, m * E:(m + 1) * E], keep["w2_l"][:, e, m * E:(m + 1) * E]
                for blk in range(NBLK):
                    t = slice(blk * P, (blk + 1) * P)
                    for k, (g_, w) in enumerate(((gh, wh), (gh, wl), (gl, wh))):
                        mm = pe.matmul(o[blk], g_[:, c % 2, t], w, start=False, stop=(m == MT - 1 and k == 2),
                                       skip_group_check=True)
                mm.then_inc(S["down_done"], 1)

            def gate(i):
                name = ("gate",)
                pe.wait_ge(*read(i, ("split_c", 3)))
                pe.wait_ge(*room(i, name))
                for blk in range(NBLK):
                    mm = tokens_by(slot(name)[:, blk * NEXP:(blk + 1) * NEXP], xparts[1], blk, keep["gw_h"][:, :],
                                   keep["gw_l"][:, :], keep["gw_c"][:, :],
                                   bias_of(BIAS_AT[2], NMLP * E, NMLP * E + NEXP))
                mm.then_inc(full_sem(name), 1)

            def ffn(i, kind, c):
                if kind == "split":
                    if c == 2:
                        for j in range(2):
                            pe.wait_ge(*ring.read(i, ("proj", j)))
                    else:
                        pe.wait_ge(*at(i, "ln4_out", 0))
                    split(i, c, y if c == 2 else xm)
                if kind == "up":
                    up(i, c)
                if kind == "down":
                    down(i, c)
                if kind == "gate":
                    gate(i)

            def attention(i, beside):
                for a in range(2):
                    beside(("start", a, 0))
                    pe.wait_ge(*at(i, "ln_out", 3 * a))
                    split(i, a, u if a == 0 else y)
                    beside(("parts", a, 0))
                    for part in "ac":
                        pe.wait_ge(*ring.read(i, ("split_" + part, a)))
                    prepare(i, a, 0, beside)
                    beside(("ready", a, 0))
                    for n in range(12):
                        maximum(i, a, 0, n)
                        if n % 3 == 2:
                            beside(("max0", a, n // 3))
                    prepare(i, a, 1, beside)
                    beside(("next", a, 0))
                    negmax(i, a, 0)
                    for n in range(12 + LAG):
                        if n < 12:
                            maximum(i, a, 1, n)
                        if n == LAG:
                            beside(("both", a, 0))
                        if n >= LAG:
                            score(i, a, 0, n - LAG)
                            if (n - LAG) % 2 and n - LAG >= 3:
                                pv(i, a, 0, (n - LAG - 3) // 2)
                        if n == NEG_AT + LAG:
                            negmax(i, a, 1)
                    pv(i, a, 0, 5)
                    beside(("mid", a, 0))
                    context(i, a, 0)
                    for n in range(12):
                        score(i, a, 1, n)
                        if n % 2 and n >= 3:
                            pv(i, a, 1, (n - 3) // 2)
                        if n == 2:
                            beside(("exp1", a, 0))
                    pv(i, a, 1, 5)
                    context(i, a, 1)
                    beside(("end", a, 0))
                for half in range(2):
                    pe.wait_ge(*ring.read(i, ("ctx", 1, 1, half)))
                for k in (1, 0):
                    pe.wait_ge(*ring.room(i, ("ctxT", k)))
                for k, c0, c1 in ((0, 0, P), (1, P, E)):
                    name = ("ctxT", k)
                    for blk in range(NBLK):
                        mm = pe.transpose(slot(name)[0:c1 - c0, blk * P:(blk + 1) * P], y[:, blk, c0:c1], ident[:, :])
                    mm.then_inc(full_sem(name), 1)
                beside(("proj", 1, 0))
                for k in range(2):
                    pe.wait_ge(*ring.read(i, ("ctxT", k)))
                for j in range(2):
                    name = ("proj", j)
                    pe.wait_ge(*ring.room(i, name))
                    for k in range(2):
                        blk = 2 * j + k
                        o = slot(name)[:, k * E:(k + 1) * E]
                        pe.matmul(o, *bias_of(BIAS_AT[0], 3 * E, 4 * E), start=True, stop=False)
                        pe.matmul(o, ctxT[0][:, blk * P:(blk + 1) * P], keep["ow_a"][:, :], start=False, stop=False)
                        mm = pe.matmul(o, ctxT[1][0:E2, blk * P:(blk + 1) * P], keep["ow_c"][:, :],
                                       start=False, stop=True)
                    mm.then_inc(full_sem(name), 1)
                beside(("over", 1, 0))

            pipeline(pe, attention, ffn)


def build(nc, a, out):
    const = {
        "scratch1": nc.dram_tensor("scratch1", [L1 * GP, B * C1], F32, kind="Internal").ap(),
        "scratch2": nc.dram_tensor("scratch2", [L2 * GP, B * C2], F32, kind="Internal").ap(),
        "h": nc.dram_tensor("h_tokens", [B * N, E], F32, kind="Internal").ap(),
    }
    shapes = {
        "ident": ([P, P], F32), "ones": ([P, P], F32R), "b1": ([P, NMLP * MT], F32), "tri": ([P, NEXP, NEXP], F32),
        "wq_h": ([P, 2, 3 * E], F32R), "wq_l": ([P, 2, 3 * E], F32R), "wq_c": ([P, 2, 3 * E], F32R),
        "bias": ([P, NMLP * E + NEXP], F32R), "gw_h": ([P, NEXP], F32R), "gw_l": ([P, NEXP], F32R),
        "gw_c": ([P, NEXP], F32R),
        "w1_h": ([P, NMLP, HID], F32R), "w1_l": ([P, NMLP, HID], F32R), "w1_c": ([P, NMLP, HID], F32R),
        "w2_h": ([P, NMLP, MT * E], F32R), "w2_l": ([P, NMLP, MT * E], F32R),
        "ow_a": ([P, E], F32), "ow_c": ([E2, E], F32),
        "ln_g1": ([P, E], F32), "ln_b1": ([P, E], F32), "ln_g3": ([P, E], F32), "ln_b3": ([P, E], F32),
        "ln_g4": ([P, E], F32), "ln_b4": ([P, E], F32),
    }
    with ExitStack() as ctx:
        keep = {name: ctx.enter_context(nc.sbuf_tensor("keep_" + name, shape, dt))
                for name, (shape, dt) in shapes.items()}
        prepare_and_tokenize(nc, a, keep, const)
        tower(nc, keep, const, out)


def interpolation(length):
    pos = (np.arange(N, dtype=np.float32) + np.float32(0.5)) * np.float32(length / N) - np.float32(0.5)
    pos = np.clip(pos, 0.0, length - 1).astype(np.float32)
    i0 = np.floor(pos).astype(np.int64)
    i1 = np.minimum(i0 + 1, length - 1)
    w = (pos - i0).astype(np.float32)
    m = np.zeros((length, N), np.float32)
    m[i0, np.arange(N)] += np.float32(1.0) - w
    m[i1, np.arange(N)] += w
    return m


def kernel(**inputs):
    import concourse.bacc as bacc
    from concourse.bass_utils import run_bass_kernel_spmd

    t = {k: np.asarray(v) for k, v in inputs.items()}
    g = lambda name: t["L0_" + name]
    xin = t["x"]
    put = {}
    for k, p in enumerate(PRE):
        n = IMG // p
        put[f"x{k}r"] = xin.reshape(B, CH, n, p, n, p).transpose(2, 4, 0, 3, 5, 1).reshape(n * n, B * CH * p * p)
        if p == 1:
            put["x0r"] = xin.transpose(2, 3, 1, 0).reshape(n * n, CH * B)
    put["idx0"] = g("tok_idx0").reshape(2, P, GP).transpose(1, 0, 2)
    put["idx1"] = g("tok_idx1").reshape(8, P).T
    put["idx2"] = g("tok_idx2").reshape(2, P).T
    put["w0T"] = g("tok_W0").T
    put["w1T"] = g("tok_W1").T.reshape(2, 96, EMB).transpose(1, 0, 2)
    put["w2T"] = g("tok_W2").T.reshape(6, P, EMB).transpose(1, 0, 2)
    put["wfT"] = g("tok_Wf").T.reshape(3, EMB, E).transpose(1, 0, 2)
    put["tb"] = np.stack([g("tok_b0"), g("tok_b1"), g("tok_b2")], 1)
    put["bf"] = g("tok_bf")
    put["interp1"] = interpolation(L1)
    m2, two = interpolation(L2), np.zeros((4, 2, L2, 2, N), np.float32)
    for r in range(2):
        two[:, r, :, r, :] = m2
    put["interp2"] = two.reshape(P, 2, N)
    put["wqkv"] = np.stack([g("attn_w_qkv"), g("ffn_in_w").T])
    put["bqkv"] = np.stack([g("attn_b_qkv"), g("ffn_in_b")])
    put["g1"], put["be1"] = g("attn_ln_gamma"), g("attn_ln_beta")
    put["g3"], put["be3"] = g("ffn_ln1_g"), g("ffn_ln1_b")
    put["g4"], put["be4"] = g("ffn_ln2_g"), g("ffn_ln2_b")
    put["owT"], put["ob"] = g("ffn_out_w").T, g("ffn_out_b").reshape(1, E)
    put["gate_wT"], put["gate_b"] = g("ffn_gate_w").T, g("ffn_gate_b").reshape(1, NEXP)
    put["w1"] = np.concatenate([g("ffn_mlp_w1")[None], g("ffn_exp_w1")])
    put["b1"] = np.concatenate([g("ffn_mlp_b1")[None], g("ffn_exp_b1")]).reshape(NMLP * MT, P).T
    w2 = np.concatenate([g("ffn_mlp_w2")[None], g("ffn_exp_w2")])
    put["w2"] = w2.reshape(NMLP, MT, P, E).transpose(2, 0, 1, 3).reshape(P, NMLP, MT * E)
    put["b2"] = np.concatenate([g("ffn_mlp_b2")[None], g("ffn_exp_b2")]).reshape(1, NMLP * E)
    put["tri"] = np.tril(np.ones((NEXP, NEXP), np.float32), -1)

    nc = bacc.Bacc("TRN2", target_bir_lowering=False, num_devices=1)
    put = {k: np.ascontiguousarray(v) for k, v in put.items()}
    aps = {k: nc.dram_tensor("in_" + k, v.shape, mybir.dt.from_np(v.dtype), kind="ExternalInput").ap()
           for k, v in put.items()}
    out = nc.dram_tensor("out", (B, N, E), F32, kind="ExternalOutput").ap()
    build(nc, aps, out)
    r = run_bass_kernel_spmd(nc, [{"in_" + k: v for k, v in put.items()}], core_ids=[0])
    return r.results[0]["out"]
```

```python
from contextlib import ExitStack

import concourse.bass as bass
import numpy as np
from concourse import mybir

F32 = mybir.dt.float32
F32R = mybir.dt.float32r
I32 = mybir.dt.int32
ALU = mybir.AluOpType
ACT = mybir.ActivationFunctionType
AX = mybir.AxisListType

P = 128
B, CH, IMG = 16, 3, 64
GP = 16
PRE = (1, 2, 4)
N = IMG * IMG // GP
L1, L2 = N // 4, N // 16
C0, C1, C2 = (CH * p * p for p in PRE)
EMB = 64
E = 3 * EMB
E2 = E - P
H, D = 12, 16
HP = H // 2
DS = 64
HID = 768
MT = HID // P
NEXP = 4
NMLP = 1 + NEXP
EPS = 1e-5
PAIR = 2
T = PAIR * N
NBLK = T // P
NIT = B // PAIR
MAGIC = float(0x5F3759DF)
NEWTON = 3
BIAS_AT = (0, 32, 64)


def ev(i, per, n):
    return (i + 1) * per + n + 1


class Ring:

    def __init__(self, products, full, read):
        self.full_sem, self.read_sem = full, read
        self.slot = {name: k % len(full) for k, name in enumerate(products)}
        self.nth = {name: k // len(full) for k, name in enumerate(products)}
        self.per = [sum(s == k for s in self.slot.values()) for k in range(len(full))]

    def full(self, i, name):
        s = self.slot[name]
        return self.full_sem[s], ev(i, self.per[s], self.nth[name])

    def read(self, i, name):
        s = self.slot[name]
        return self.read_sem[s], ev(i, self.per[s], self.nth[name])

    def room(self, i, name):
        s = self.slot[name]
        return self.read_sem[s], ev(i, self.per[s], self.nth[name] - 1)



def ring_products():
    def prepare(a, b):
        return ([("qk", a, b, 0), ("qk", a, b, 1), ("v", a, b)] + [("negmax", a, 0)] * b
                + [(x, a, b, g) for x in "kq" for g in range(3)])

    out = []
    for a in range(2):
        out += [("split_a", a), ("split_c", a)] + prepare(a, 0)
        out += [("max", a, 0, n) for n in range(12)] + prepare(a, 1)
        for n in range(12 + LAG):
            out += [("max", a, 1, n)] * (n < 12) + [("score", a, 0, n - LAG)] * (n >= LAG)
            out += [("negmax", a, 1)] * (n == NEG_AT + LAG)
        out += [("ctx", a, 0, 0), ("ctx", a, 0, 1)]
        out += [("score", a, 1, n) for n in range(12)] + [("ctx", a, 1, 0), ("ctx", a, 1, 1)]
    return out + [("ctxT", 0), ("ctxT", 1), ("proj", 0), ("proj", 1)]


def hid_products():
    out = [("split_a", 2), ("split_c", 2)] + [("up", c) for c in range(MT)]
    return out + [("split_a", 3), ("split_c", 3), ("gate",)] + [("up", c) for c in range(MT, MT * NMLP)]


def prepare_and_tokenize(nc, a, keep, const):
    with ExitStack() as ctx:
        sb = lambda name, shape, dt=F32: ctx.enter_context(nc.sbuf_tensor(name, shape, dt))
        sem = lambda name: ctx.enter_context(nc.semaphore(name))
        bank = [ctx.enter_context(nc.psum_tensor(f"tok_bank{k}", [P, 512], F32)) for k in range(8)]

        ident = keep["ident"]
        idx0 = sb("idx0", [P, 2, GP], I32)
        idx1 = sb("idx1", [P, 8], I32)
        idx2 = sb("idx2", [P, 2], I32)
        g0 = sb("g0", [P, 2, GP, B * C0])
        g12 = sb("g12", [P, 2 * 8 * B * C1])
        g1 = g12[:, 0:8 * B * C1].rearrange("p (m n) -> p m n", m=8)
        g2 = g12[:, 8 * B * C1:].rearrange("p (m n) -> p m n", m=2)
        x1T = g12[0:96, 0:2 * B * L1].rearrange("p (q n) -> p q n", q=2)
        x2T = g12[:, 8 * B * C1:].rearrange("p (q n) -> p q n", q=6)
        x1 = sb("x1tok", [P, 8, GP * C1])
        x2 = sb("x2tok", [P, 2, GP * C2])
        x0 = sb("x0T", [P, 2, 512])
        x0T, int2_raw = x0[0:GP * C0], x0[:, 0, :].rearrange("p (r n) -> p r n", r=2)
        y0I = sb("y0I", [P, 2, 512], F32R)
        y0l = sb("y0l", [EMB, 2, 512], F32R)
        y1 = sb("y1T", [P, B * L1])
        y1T, interp_raw = y1[0:EMB, :], y1[EMB:P, 0:N]
        y2T = sb("y2T", [EMB, B * L2])
        wfa_h, wfa_l = sb("wfa_h", [P, 2, 4, E], F32R), sb("wfa_l", [P, 2, 4, E], F32R)
        raw = sb("raw", [P, 2, MT * E])
        rawc = sb("rawc", [P, 2, HID])
        a2h, a2l = sb("a2h", [P, 2, E], F32R), sb("a2l", [P, 2, E], F32R)
        int2 = sb("int2", [P, 2, N], F32R)
        w0T = sb("w0T", [GP * C0, EMB])
        w1T = sb("w1T", [96, 2, EMB])
        w2T = sb("w2T", [P, 6, EMB])
        wfT = sb("wfT", [EMB, 3, E])
        tb = sb("tb", [EMB, 3])
        bfb = sb("bfb", [P, E])
        HB = 3
        hout = sb("hout", [P, HB, 2, E])

        idx_in, tok_in, const_in = sem("idx_in"), sem("tok_in"), sem("const_in")
        gathered0, gathered1, gathered2 = [sem("gathered0a"), sem("gathered0b")], sem("gathered1"), sem("gathered2")
        scratch_out, x1_in, x2_in = sem("scratch_out"), sem("x1_in"), sem("x2_in")
        hi_done, lo_done, act_hi = sem("hi_done"), sem("lo_done"), sem("act_hi")
        ident0, ident_done = sem("ident0"), sem("ident_done")
        tr_done, tr_evac = sem("tr_done"), sem("tr_evac")
        h_out = [sem(f"h_out{k}") for k in range(HB)]
        rows_in, rows_done, ones_done, row_out = sem("rows_in"), sem("rows_done"), sem("ones_done"), sem("row_out")
        block = ctx.enter_context(nc.Block())

        s1, s2 = const["scratch1"], const["scratch2"]

        pieces = []
        for l in range(2):
            pieces.append(("wide", a["wqkv"][l, 0:P, :], keep["wq_h"][:, l, :], keep["wq_l"][:, l, :], 3 * E))
            pieces.append(("tail", a["wqkv"][l, P:E, :], keep["wq_c"][:, l, :], None, 3 * E))
        pieces.append(("wide", a["gate_wT"][0:P, :], keep["gw_h"][:, :], keep["gw_l"][:, :], NEXP))
        pieces.append(("tail", a["gate_wT"][P:E, :], keep["gw_c"][:, :], None, NEXP))
        for e in range(NMLP):
            pieces.append(("wide", a["w1"][e, 0:P, :], keep["w1_h"][:, e, :], keep["w1_l"][:, e, :], HID))
            pieces.append(("tail", a["w1"][e, P:E, :], keep["w1_c"][:, e, :], None, HID))
            pieces.append(("wide", a["w2"][:, e, :], keep["w2_h"][:, e, :], keep["w2_l"][:, e, :], MT * E))
        stage = []
        for k, (kind, _, _, _, n) in enumerate(pieces):
            t = raw if kind == "wide" else rawc
            stage.append(t[:, sum(pieces[j][0] == kind for j in range(k)) % 2, 0:n])
        before = []
        for k, (kind, *_) in enumerate(pieces):
            same = [j for j in range(k) if pieces[j][0] == kind]
            before.append(same[-2] if len(same) >= 2 else None)
        raws = [sem(f"raw_{k}") for k in range(4)]
        part, turn = [], {}
        for k, (kind, *_) in enumerate(pieces):
            c = (kind == "tail") * 2 + sum(pieces[j][0] == kind for j in range(k)) % 2
            turn[c] = turn.get(c, 0) + (16 if kind == "wide" else 32)
            part.append((raws[c], turn[c]))

        rb = keep["bias"]
        hrow = lambda q: hout[q:q + 1].rearrange("p a b c -> p (a b c)")
        bias_rows = [(rb[q:q + 2, 0:3 * E], a["bqkv"][l:l + 1, :], hrow(q)[:, 0:3 * E])
                     for l, q in enumerate(BIAS_AT[:2])]
        bias_rows.append((rb[0:2, 3 * E:4 * E], a["ob"], hrow(0)[:, 3 * E:4 * E]))
        q = BIAS_AT[2]
        bias_rows += [(rb[q:q + 2, 0:NMLP * E], a["b2"], hrow(q)[:, 0:NMLP * E]),
                      (rb[q:q + 2, NMLP * E:], a["gate_b"], hrow(q)[:, NMLP * E:NMLP * E + NEXP])]

        steps = ([("x2T", c) for c in range(3)] + [("y2", 0)] + [("x1T", c) for c in range(4)]
                 + [("y1", c) for c in range(2)] + [("a2", 0)])
        fused = len(steps)
        steps += [("x0T", 0), ("x0T", 1), ("a1", 0), ("a1", 1), ("y0", 0)]
        for q in range(8):
            steps += [("x0T", q + 2)] * (q < 6) + [("a1", q + 1), ("a1", q + 2)] * (q % 2 == 1 and q < 7)
            steps += [("y0", q + 1)] * (q < 7) + [("h", q, 0), ("h", q, 1)]
        with_hi = [s for s in steps if s[0] in ("a2", "a1", "y0")]
        hi_count = {s: 2 + n for n, s in enumerate(with_hi)}
        before_step = {0: 7, 4: 5, 8: 3, 9: 2, 10: 1, 11: 1, 12: 1, 15: 1}
        weights_before, k = {}, 0
        for n, count in before_step.items():
            weights_before[n] = range(k, k + count)
            k += count
        assert k == len(pieces)
        order = {s: n for n, s in enumerate(steps)}

        @block.sync
        def _(sp):
            sp.dma_start(idx2[:, :], a["idx2"]).then_inc(idx_in, 16)
            sp.dma_start(idx1[:, :], a["idx1"]).then_inc(idx_in, 16)
            sp.dma_start(idx0[:, :, :], a["idx0"]).then_inc(idx_in, 16)
            for _, src, row in bias_rows:
                sp.dma_start(row, src).then_inc(rows_in, 16)
            for dst, src in ((w2T[:, :, :], a["w2T"]), (w1T[:, :, :], a["w1T"]), (wfT[:, :, :], a["wfT"]),
                             (tb[:, :], a["tb"]), (w0T[:, :], a["w0T"]),
                             (bfb[:, :], a["bf"].partition_broadcast(P)), (int2_raw, a["interp2"]),
                             (interp_raw, a["interp1"])):
                sp.dma_start(dst, src).then_inc(tok_in, 16)
            sp.wait_ge(gathered2, 32)
            for m in range(2):
                sp.dma_start(s2.rearrange("b (m p) c -> m p b c", p=P)[m],
                             g2[:, m, :].rearrange("p (b c) -> p b c", b=B))\
                    .then_inc(scratch_out, 16)
            sp.wait_ge(scratch_out, 16 * 2)
            sp.dma_start(x2[:, :, :], s2.rearrange("b q c -> (b q c)").rearrange("(r p n) -> p r n", p=P, r=2))\
                .then_inc(x2_in, 16)
            sp.wait_ge(gathered1, 8 * 16)
            for m in range(8):
                sp.dma_start(s1.rearrange("b (m p) c -> m p b c", p=P)[m],
                             g1[:, m, :].rearrange("p (b c) -> p b c", b=B))\
                    .then_inc(scratch_out, 16)
            sp.wait_ge(scratch_out, 16 * 10)
            sp.dma_start(x1[:, :, :], s1.rearrange("b q c -> (b q c)").rearrange("(r p n) -> p r n", p=P, r=8))\
                .then_inc(x1_in, 16)
            sp.wait_ge(rows_done, 2)
            for dst, _, row in bias_rows:
                sp.dma_start(dst[1:2].bitcast(F32), row).then_inc(row_out, 16)
            for n, (q, j) in enumerate((q, j) for q in range(8) for j in range(2)):
                c, half = q // 2, q % 2
                sp.wait_ge(tr_evac, order[("h", q, j)] + 1)
                for r in range(2):
                    b = 4 * c + 2 * j + r
                    sp.dma_start(const["h"][b * N + half * P:b * N + (half + 1) * P, :], hout[:, n % HB, r, :])\
                        .then_inc(h_out[n % HB], 16)
            for c in range(HB):
                sp.wait_ge(h_out[c], 32 * ((16 - c + HB - 1) // HB))
            sp.wait_ge(row_out, 16 * len(bias_rows))

        @block.scalar
        def _(act):
            def load(k):
                kind, src = pieces[k][:2]
                if before[k] is not None:
                    act.wait_ge(lo_done, before[k] + 1)
                if kind == "wide":
                    act.dma_start(stage[k], src).then_inc(part[k][0], 16)
                else:
                    act.dma_start(stage[k][0:E2], src).then_inc(part[k][0], 16)
                    act.dma_start(stage[k][E2:P], src).then_inc(part[k][0], 16)

            AHEAD = 3
            for k in range(AHEAD):
                load(k)
            def split_hi(k):
                act.wait_ge(*part[k])
                act.copy(pieces[k][2], stage[k]).then_inc(hi_done, 1)
                if k + AHEAD < len(pieces):
                    load(k + AHEAD)

            for dst, src in ((keep["b1"][:, :], a["b1"]), (keep["ln_g1"][:, :], a["g1"].partition_broadcast(P)),
                             (keep["ln_b1"][:, :], a["be1"].partition_broadcast(P)),
                             (keep["ln_g3"][:, :], a["g3"].partition_broadcast(P)),
                             (keep["ln_b3"][:, :], a["be3"].partition_broadcast(P)),
                             (keep["ln_g4"][:, :], a["g4"].partition_broadcast(P)),
                             (keep["ln_b4"][:, :], a["be4"].partition_broadcast(P)),
                             (keep["ow_a"][:, :], a["owT"][0:P, :]), (keep["ow_c"][:, :], a["owT"][P:E, :]),
                             (keep["tri"][:, :, :], a["tri"].partition_broadcast(P))):
                act.dma_start(dst, src).then_inc(const_in, 16)
            for step in steps:
                n = order[step]
                src = bank[n % 8]
                for k in weights_before.get(n, ()):
                    split_hi(k)
                if n == 0:
                    act.wait_ge(tok_in, 16 * 8)
                    act.copy(wfa_h[0:EMB, :, :, :].rearrange("p a b e -> p (a b) e"),
                             wfT[:, 0, :].unsqueeze(1).to_broadcast([EMB, 8, E])).then_inc(act_hi, 1)
                if step[0] in ("a2", "a1", "y0"):
                    act.wait_ge(tr_done, n + 1)
                if step[0] == "a2":
                    act.copy(a2h[:, :, :], src[:, 0:2 * E].rearrange("p (r n) -> p r n", r=2)).then_inc(act_hi, 1)
                if step[0] == "a1":
                    c = step[1]
                    act.copy(wfa_h[EMB:P, c // 2 % 2, 2 * (c % 2):2 * (c % 2) + 2, :],
                             src[EMB:P, 0:2 * E].rearrange("p (r n) -> p r n", r=2)).then_inc(act_hi, 1)
                if step[0] == "y0":
                    act.activation(y0I[0:EMB, step[1] % 2, :], src[0:EMB, :], ACT.Identity, bias=tb[:, 0:1])\
                       .then_inc(act_hi, 1)
            act.wait_ge(const_in, 16 * 10)

        @block.gpsimd
        def _(pool):
            pool.wait_ge(idx_in, 48)
            for m in range(2):
                pool.indirect_dma_start(out=g2[:, m, :], out_offset=None, in_=a["x2r"],
                                        in_offset=bass.IndirectOffsetOnAxis(ap=idx2[:, m:m + 1], axis=0))\
                    .then_inc(gathered2, 16)
            pool.memset(ident[:, :], 0.0).then_inc(ident0, 1)
            pool.wait_ge(ident0, 1)
            pool.affine_select(out=ident[:, :], in_=ident[:, :], compare_op=ALU.not_equal, fill=1.0,
                               base=0, pattern=[[-1, P]], channel_multiplier=1).then_inc(ident_done, 1)
            for m in range(8):
                pool.indirect_dma_start(out=g1[:, m, :], out_offset=None, in_=a["x1r"],
                                        in_offset=bass.IndirectOffsetOnAxis(ap=idx1[:, m:m + 1], axis=0))\
                    .then_inc(gathered1, 16)
            for blk in range(2):
                for j in range(GP):
                    pool.indirect_dma_start(out=g0[:, blk, j, :], out_offset=None, in_=a["x0r"],
                                            in_offset=bass.IndirectOffsetOnAxis(ap=idx0[:, blk, j:j + 1], axis=0))\
                        .then_inc(gathered0[blk], 16)

        @block.tensor
        def _(pe):
            pe.wait_ge(ident_done, 1)
            pe.wait_ge(tok_in, 16 * 8)

            def out(step):
                n = order[step]
                if n >= 8:
                    pe.wait_ge(tr_evac, n - 7)
                return bank[n % 8]

            pe.wait_ge(x2_in, 16)
            for c in range(3):
                o = out(("x2T", c))
                for k in range(4):
                    q, r = (4 * c + k) // 2, k % 2
                    mm = pe.transpose(o[:, k * P:(k + 1) * P], x2[:, r, q * P:(q + 1) * P], ident[:, :])
                mm.then_inc(tr_done, 1)
            pe.wait_ge(tr_evac, 3)
            o = out(("y2", 0))
            for q in range(6):
                mm = pe.matmul(o[0:EMB, 0:B * L2], w2T[:, q, :], x2T[:, q, :], start=(q == 0), stop=(q == 5))
            mm.then_inc(tr_done, 1)
            pe.wait_ge(x1_in, 16)
            for c in range(4):
                o = out(("x1T", c))
                for k in range(4):
                    q, r = c // 2, (c % 2) * 4 + k
                    mm = pe.transpose(o[0:96, k * P:(k + 1) * P], x1[:, r, q * 96:(q + 1) * 96], ident[:, :])
                mm.then_inc(tr_done, 1)
            pe.wait_ge(tr_evac, 8)
            for c in range(2):
                o = out(("y1", c))
                for q in range(2):
                    mm = pe.matmul(o[0:EMB, :], w1T[:, q, :], x1T[:, q, c * 512:(c + 1) * 512],
                                   start=(q == 0), stop=(q == 1))
                mm.then_inc(tr_done, 1)
            pe.wait_ge(tr_evac, 10)
            o = out(("a2", 0))
            for r in range(2):
                mm = pe.matmul(o[:, r * E:(r + 1) * E], y2T[:, r * P:(r + 1) * P], wfT[:, 2, :], start=True, stop=True)
            mm.then_inc(tr_done, 1)
            for step in steps[fused:]:
                c, half = step[1] // 2, step[1] % 2
                o = out(step)
                if step[0] == "a1":
                    for r in range(2):
                        b = 2 * step[1] + r
                        mm = pe.matmul(o[EMB:P, r * E:(r + 1) * E], y1T[:, b * L1:(b + 1) * L1], wfT[:, 1, :],
                                       start=True, stop=True)
                if step[0] == "x0T":
                    if c == 0:
                        pe.wait_ge(gathered0[half], 16 * GP)
                    for k in range(4):
                        b = 4 * c + k
                        mm = pe.transpose(o[0:GP * C0, k * P:(k + 1) * P],
                                          g0[:, half].rearrange("p j n -> p (j n)")[:, b::B], ident[:, :])
                if step[0] == "y0":
                    pe.wait_ge(tr_evac, order[("x0T", step[1])] + 1)
                    mm = pe.matmul(o[0:EMB, :], w0T[:, :], x0T[:, half, :], start=True, stop=True)
                if step[0] == "h":
                    pe.wait_ge(tr_evac, order[("y0", step[1])] + 1)
                    for r in range(2):
                        b = 4 * c + 2 * step[2] + r
                        g, t = 32 * (b % 8 // 2), slice((b % 4) * P, (b % 4 + 1) * P)
                        ob = o[:, r * E:(r + 1) * E]
                        y0b = y0I[:, half, t]
                        pe.matmul(ob, y0b, wfa_h[:, c % 2, b % 4, :], start=True, stop=False)
                        pe.matmul(ob, y0b, wfa_l[:, c % 2, b % 4, :], start=False, stop=False)
                        pe.matmul(ob, y0l[:, half, t], wfa_h[0:EMB, c % 2, b % 4, :], start=False, stop=False)
                        i2 = int2[g:g + 32, b % 2, half * P:(half + 1) * P]
                        pe.matmul(ob, i2, a2h[g:g + 32, b // 8, :], start=False, stop=False)
                        mm = pe.matmul(ob, i2, a2l[g:g + 32, b // 8, :], start=False, stop=True)
                mm.then_inc(tr_done, 1)

        @block.vector
        def _(dve):
            dve.memset(keep["ones"][:, :].bitcast(F32), 1.0).then_inc(ones_done, 1)
            dve.wait_ge(rows_in, 16 * len(bias_rows))
            for dst, _, row in bias_rows:
                ins = dve.tensor_copy(dst[0:1], row)
            ins.then_inc(rows_done, 1)
            dve.wait_ge(rows_done, 1)
            for dst, _, row in bias_rows:
                ins = dve.tensor_tensor(row, row, dst[0:1].bitcast(F32), ALU.subtract)
            ins.then_inc(rows_done, 1)

            def split(k):
                kind, _, hi, lo, n = pieces[k]
                dve.wait_ge(hi_done, k + 1)
                if kind == "wide":
                    dve.tensor_tensor(lo, stage[k], hi.bitcast(F32), ALU.subtract).then_inc(lo_done, 1)
                else:
                    dve.tensor_tensor(hi[E2:P], stage[k][E2:P], hi[E2:P].bitcast(F32), ALU.subtract)\
                       .then_inc(lo_done, 1)

            def evac(step):
                n = order[step]
                src = bank[n % 8]
                dve.wait_ge(tr_done, n + 1)
                kind = step[0]
                if kind == "x2T":
                    c = step[1]
                    ins = dve.tensor_copy(x2T[:, 2 * c:2 * c + 2, :].rearrange("p q n -> p (q n)"), src[:, :])
                elif kind == "y2":
                    ins = dve.tensor_scalar(y2T[:, :], src[0:EMB, 0:B * L2], tb[:, 2:3], None, ALU.add)
                elif kind == "x1T":
                    c = step[1]
                    ins = dve.tensor_copy(x1T[:, c // 2, (c % 2) * 512:(c % 2 + 1) * 512], src[0:96, :])
                elif kind == "y1":
                    ins = dve.tensor_scalar(y1T[:, step[1] * 512:(step[1] + 1) * 512], src[0:EMB, :],
                                            tb[:, 1:2], None, ALU.add)
                elif kind == "a2":
                    dve.wait_ge(act_hi, hi_count[step])
                    ins = dve.tensor_tensor(a2l[:, :, :], src[:, 0:2 * E].rearrange("p (r n) -> p r n", r=2),
                                            a2h[:, :, :].bitcast(F32), ALU.subtract)
                elif kind == "a1":
                    c = step[1]
                    dve.wait_ge(act_hi, hi_count[step])
                    k = c // 2 % 2, slice(2 * (c % 2), 2 * (c % 2) + 2)
                    ins = dve.tensor_tensor(wfa_l[EMB:P, k[0], k[1], :],
                                            src[EMB:P, 0:2 * E].rearrange("p (r n) -> p r n", r=2),
                                            wfa_h[EMB:P, k[0], k[1], :].bitcast(F32), ALU.subtract)
                elif kind == "x0T":
                    ins = dve.tensor_copy(x0T[:, step[1] % 2, :], src[0:GP * C0, :])
                elif kind == "y0":
                    half = step[1] % 2
                    dve.wait_ge(act_hi, hi_count[step])
                    ins = dve.scalar_tensor_tensor(out=y0l[:, half, :], in0=src[0:EMB, :], scalar=tb[:, 0:1],
                                                   in1=y0I[0:EMB, half, :].bitcast(F32), op0=ALU.add,
                                                   op1=ALU.subtract)
                else:
                    n_h = 2 * step[1] + step[2]
                    if n_h >= HB:
                        dve.wait_ge(h_out[n_h % HB], 32 * (n_h // HB))
                    for r in range(2):
                        ins = dve.tensor_tensor(hout[:, n_h % HB, r, :], src[:, r * E:(r + 1) * E], bfb[:, :], ALU.add)
                ins.then_inc(tr_evac, 1)

            dve.wait_ge(tok_in, 16 * 8)
            dve.tensor_copy(int2[:, :, :], int2_raw)
            for half in range(2):
                dve.tensor_copy(y0I[EMB:P, half, :].rearrange("p (b n) -> p b n", b=4),
                                interp_raw[:, half * P:(half + 1) * P].unsqueeze(1).to_broadcast([EMB, 4, P]))
            for step in steps:
                n = order[step]
                for k in weights_before.get(n, ()):
                    split(k)
                if n == 4:
                    dve.wait_ge(act_hi, 1)
                    dve.tensor_tensor(wfa_l[0:EMB, :, :, :].rearrange("p a b e -> p (a b) e"),
                                      wfT[:, 0, :].unsqueeze(1).to_broadcast([EMB, 8, E]),
                                      wfa_h[0:EMB, :, :, :].rearrange("p a b e -> p (a b) e").bitcast(F32),
                                      ALU.subtract)
                if step[0] == "h" and step[1:] == (0, 0):
                    dve.wait_ge(row_out, 16 * len(bias_rows))
                evac(step)


NEG_AT = 10
LAG = 2
REST = 99
BESIDE = [
    ("start", 0, 6), ("parts", 0, 3), ("heads0", 0, 1), ("ready", 0, 1),
    *[("max0", 0, n) for n in (1, 1, 0, 2)], ("heads1", 0, 1), ("next", 0, 4), ("both", 0, 1), ("mid", 0, 1),
    ("exp1", 0, 0), ("end", 0, 5),
    ("start", 1, 2), ("chain1", 1, 4), ("chain2", 1, 8), ("parts", 1, 1), ("heads0", 1, 2), ("ready", 1, 1),
    *[("max0", 1, n) for n in (3, 2, 2, 2)], ("heads1", 1, 2), ("next", 1, 0), ("both", 1, 1), ("mid", 1, 2),
    ("exp1", 1, 0), ("end", 1, 1), ("proj", 1, 2), ("over", 1, REST),
]


def ffn_steps():
    def tiles(c0, c1):
        out = [("up", c0)]
        for c in range(c0 + 1, c1):
            out += [("up", c), ("down", c - 1)]
        return out + [("down", c1 - 1)]

    return ([("split", 2)] + tiles(0, MT) + [("sum", 0), ("stats", 4), ("norm", 4), ("split", 3), ("gate", 0)]
            + tiles(MT, MT * NMLP)
            + [("last", 0)])


def place_steps():
    steps, at_point, seen = ffn_steps(), {}, {}
    for phase, layer, count in BESIDE:
        n = seen[phase, layer] = seen.get((phase, layer), -1) + 1
        at_point[phase, layer, n], steps = steps[:count], steps[count:]
    assert not steps
    return at_point


def tower(nc, keep, const, out):
    with ExitStack() as ctx:
        sb = lambda name, shape, dt=F32: ctx.enter_context(nc.sbuf_tensor(name, shape, dt))
        sem = lambda name: ctx.enter_context(nc.semaphore(name))
        pb = lambda name: ctx.enter_context(nc.psum_tensor(name, [P, 512], F32))

        NR, NPROB = 3, 4
        ring_bank = [pb(f"ring{k}") for k in range(NR)]
        ctx_bank = pb("ctx_bank")
        hid_bank = [pb("hid_bank0"), pb("hid_bank1")]
        mlp_bank = [pb("mlp_bank0"), pb("mlp_bank1")]
        ident = keep["ident"]

        h = sb("h", [P, NBLK, E])
        u = sb("u", [P, NBLK, E])
        y = sb("y", [P, NBLK, E])
        x = sb("x", [P, NBLK, E])
        xparts = [(sb(f"xh{k}", [P, T], F32R), sb(f"xl{k}", [P, T], F32R), sb(f"xch{k}", [P, T], F32R),
                   sb(f"xcl{k}", [E2, T], F32R)) for k in range(2)]
        qs, ks = sb("qs", [P, 2, H, DS]), sb("ks", [P, 2, H, DS])
        kT = [sb(f"kT{b}", [P, HP, N], F32R) for b in range(2)]
        qT = [sb(f"qT{b}", [P, HP, N], F32R) for b in range(2)]
        v = sb("v", [P, 2, 2, H, 2 * D])
        prob = sb("prob", [P, NPROB, 2, N])
        cT = sb("cT", [P, 3 * N])
        mx = sb("mx", [P, 2, 2, HP])
        ms = sb("ms", [P, 2, 2, 2, HP], F32R)
        msT = keep["bias"][96:96 + 4 * HP, 0:N]
        rsum = sb("rsum", [P, 2, H])
        st, mv1 = sb("st", [P, NBLK, 6]), sb("mv1", [P, NBLK, 2])
        mv4, yn4, hv4, tn4 = sb("mv4", [P, NBLK, 2]), *(sb(name, [P, NBLK]) for name in ("yn4", "hv4", "tn4"))
        spare = prob[:, :, :, :].rearrange("p a b n -> p (a b n)")
        fresh = spare[:, 0:NBLK * E].rearrange("p (c e) -> p c e", c=NBLK)
        ctxT = [spare[:, 2 * T:3 * T], spare[:, 3 * T:4 * T]]
        ve, yn1, hv, tn = (sb(name, [P, NBLK]) for name in ("ve", "yn1", "hv", "tn"))
        sh = sb("sh", [P, NBLK], I32)
        lg, ex = sb("lg", [P, NBLK, NEXP]), sb("ex", [P, NBLK, NEXP])
        rank, comb = sb("rank", [P, NBLK, NEXP]), sb("comb", [P, NBLK, NEXP])
        m1, s1 = sb("m1", [P, NBLK]), sb("s1", [P, NBLK])
        primer = sb("primer", [P, 7])
        gel_xm = sb("gel_xm", [P, NBLK * E])
        gel = gel_xm[:, 0:T]
        xm = gel_xm[:, :].rearrange("p (c e) -> p c e", c=NBLK)
        gt4, eq4 = (gel_xm[:, T + k * NBLK * NEXP ** 2:T + (k + 1) * NBLK * NEXP ** 2]
                    .rearrange("p (c j e) -> p c j e", c=NBLK, j=NEXP) for k in range(2))
        gh, gl = sb("gh", [P, 2, T], F32R), sb("gl", [P, 2, T], F32R)

        ring = Ring(ring_products(), [sem(f"ring_full{k}") for k in range(NR)],
                    [sem(f"ring_read{k}") for k in range(NR)])
        hid = Ring(hid_products(), [sem(f"hid_full{k}") for k in range(2)], [sem(f"hid_read{k}") for k in range(2)])
        u_in, h_in = sem("u_in"), sem("h_in")
        stored = sem("stored")
        neg_in = sem("neg_in")
        zeroed = sem("zeroed")
        passed = sem("passed")
        CHAIN = 6 + 3 * NEWTON
        PER = dict(ln_chain=CHAIN * 4, ln4_chain=6, ln_pool=4 * NEWTON, ln_affine=2, ln4_affine=1,
                   ln_out=4, ln4_out=1, y_sum=NBLK, h_sum=1,
                   res=1, hi_copy=4, fhi_copy=4, qk_hi=8, neg_hi=4, neg_done=4, pv_done=24,
                   cbank_read=12, rs_done=8, gl_done=MT * NMLP,
                   down_done=MT * NMLP, acc_read=NMLP, gate_chain=12, gate_exp=1)
        S = {name: sem(name) for name in PER}
        points = place_steps()
        block = ctx.enter_context(nc.Block())

        def at(i, name, n):
            return S[name], ev(i, PER[name], n)

        def credit(eng, *names):
            for name in names:
                eng.sem_inc(S[name], PER[name])

        def plan_of(name):
            return (ring, ring_bank) if name in ring.slot else (hid, hid_bank)

        def slot(name):
            plan, banks = plan_of(name)
            return banks[plan.slot[name]]

        def read_sem(name):
            plan, _ = plan_of(name)
            return plan.read_sem[plan.slot[name]]

        def full_sem(name):
            plan, _ = plan_of(name)
            return plan.full_sem[plan.slot[name]]

        def full(i, name):
            return plan_of(name)[0].full(i, name)

        def read(i, name):
            return plan_of(name)[0].read(i, name)

        def room(i, name):
            return plan_of(name)[0].room(i, name)

        def pipeline(eng, attention, ffn):
            attention(0, lambda point: None)
            with eng.Fori(1, NIT) as i:
                def beside(point):
                    for step in points[point]:
                        ffn(i - 1, *step)
                attention(i, beside)
            for step in ffn_steps():
                ffn(NIT - 1, *step)

        def beside_all(beside, layer, *phases):
            for point in points:
                if point[0] in phases and point[1] == layer:
                    beside(point)

        @block.sync
        def _(sp):
            sp.sem_inc(stored, 16)
            sp.sem_inc(neg_in, 4 * 64)
            hd = const["h"].rearrange("(i c p) e -> i p c e", p=P, c=NBLK)
            od = out.rearrange("b n e -> (b n) e").rearrange("(i c p) e -> i p c e", p=P, c=NBLK)

            def attention(i, beside):
                src = hd[i]
                sp.wait_ge(*at(i - 1, "pv_done", PER["pv_done"] - 1))
                sp.dma_start(fresh, src).then_inc(u_in, 16)
                if isinstance(i, int):
                    sp.dma_start(h[:, :, :], src).then_inc(h_in, 16)
                for a in range(2):
                    beside_all(beside, a, "start", "chain1", "chain2", "parts", "heads0", "ready", "max0")
                    for b in range(2):
                        sp.wait_ge(*ring.read(i, ("negmax", a, b)))
                        for p in range(2):
                            for r in range(2):
                                row = 64 * p + 3 * D + r
                                sp.dma_start(qT[b][row:row + 1, :, :].bitcast(F32),
                                             msT[(2 * p + r) * HP:(2 * p + r + 1) * HP, :].bitcast(F32)).then_inc(neg_in, 16)
                        if b == 0:
                            beside_all(beside, a, "heads1", "next", "both")
                    beside_all(beside, a, "mid", "exp1", "end", "proj", "over")

            def ffn(i, kind, c):
                if kind == "split" and c == 3 and not isinstance(i, int):
                    src = hd[i + 1]
                    sp.wait_ge(*at(i, "res", 0))
                    sp.dma_start(h[:, :, :], src).then_inc(h_in, 16)
                if kind == "last":
                    dst = od[i]
                    sp.wait_ge(*at(i, "acc_read", NMLP - 1))
                    sp.dma_start(dst, x[:, :, :]).then_inc(stored, 16)

            pipeline(sp, attention, ffn)
            sp.wait_ge(stored, 16 * (NIT + 1))

        @block.gpsimd
        def _(pool):
            pool.memset(v[:, :, :, :, :], 0.0).then_inc(zeroed, 1)
            pool.memset(qs[:, :, :, :], 0.0).then_inc(zeroed, 1)
            pool.memset(ks[:, :, :, :], 0.0).then_inc(zeroed, 1)
            pool.wait_ge(zeroed, 3)
            pool.memset(v[:, :, :, :, D:D + 1], 1.0).then_inc(zeroed, 1)
            pool.memset(primer[:, :], 0.0).then_inc(zeroed, 1)
            pool.memset(ks[:, :, :, 3 * D:3 * D + 2], 1.0).then_inc(zeroed, 1)
            credit(pool, "y_sum", "res", "gl_done", "ln_pool")

            def attention(i, beside):
                for a in range(2):
                    beside_all(beside, a, "start", "chain1", "chain2", "parts", "heads0", "ready", "max0", "heads1", "next", "both",
                               "mid")
                    if a == 1:
                        beside_all(beside, a, "exp1", "end", "proj", "over")
                        break
                    for b in range(2):
                        if b == 1:
                            beside_all(beside, a, "exp1")
                        for half in range(2):
                            pool.wait_ge(*ring.read(i, ("ctx", 0, b, half)))
                            pool.tensor_tensor(y[:, 2 * b + half], y[:, 2 * b + half], u[:, 2 * b + half], ALU.add)\
                                .then_inc(S["y_sum"], 1)
                    beside_all(beside, a, "end")

            def ffn(i, kind, c):
                if kind == "up":
                    pool.wait_ge(*hid.read(i, ("up", c)))
                    pool.tensor_tensor(gl[:, c % 2], gel, gh[:, c % 2].bitcast(F32), ALU.subtract)\
                        .then_inc(S["gl_done"], 1)
                if kind == "stats":
                    pool.wait_ge(*at(i, "ln4_chain", 5))
                    for n in range(0, 4 * NEWTON, 4):
                        pool.tensor_tensor(tn4[:, :], yn4[:, :], yn4[:, :], ALU.mult).then_inc(S["ln_pool"], 1)
                        pool.wait_ge(*at(i, "ln_pool", n))
                        pool.tensor_tensor(tn4[:, :], tn4[:, :], hv4[:, :], ALU.mult).then_inc(S["ln_pool"], 1)
                        pool.wait_ge(*at(i, "ln_pool", n + 1))
                        pool.sem_inc(passed, 1)
                        pool.tensor_scalar(tn4[:, :], tn4[:, :], 1.5, None, ALU.add).then_inc(S["ln_pool"], 1)
                        pool.wait_ge(*at(i, "ln_pool", n + 2))
                        pool.tensor_tensor(yn4[:, :], yn4[:, :], tn4[:, :], ALU.mult).then_inc(S["ln_pool"], 1)
                        pool.wait_ge(*at(i, "ln_pool", n + 3))
                if kind == "split" and c == 3:
                    pool.wait_ge(*at(i, "ln4_out", 0))
                    pool.tensor_tensor(x[:, :, :], x[:, :, :], h[:, :, :], ALU.add).then_inc(S["res"], 1)

            pipeline(pool, attention, ffn)

        @block.scalar
        def _(act):
            act.wait_ge(zeroed, 6)
            credit(act, "hi_copy", "fhi_copy", "qk_hi", "cbank_read", "gate_exp")

            def prime(function, place):
                act.activation(primer[:, place:place + 1], primer[:, 0:1], function)

            def split_hi(i, s):
                xh, _, xch, _ = xparts[s // 2]
                done = S["fhi_copy" if s >= 2 else "hi_copy"]
                name = ("split_a", s)
                act.wait_ge(*full(i, name))
                act.copy(xh[:, :], slot(name)[:, :]).then_inc(done, 1)
                name = ("split_c", s)
                act.wait_ge(*full(i, name))
                act.copy(xch[0:E2, :], slot(name)[0:E2, :])
                act.copy(xch[E2:P, :], slot(name)[0:E2, :]).then_inc(done, 1)

            def prepare(i, a, b, beside):
                for half in range(2):
                    name = ("qk", a, b, half)
                    act.wait_ge(*ring.full(i, name))
                    src = slot(name)[:, 0:2 * E].rearrange("p (x h d) -> p x h d", x=2, h=H)
                    q2 = qs[:, half, :, 0:2 * D].rearrange("p h (r d) -> p h r d", r=2)
                    k2 = ks[:, half].rearrange("p h (r d) -> p h r d", r=2)[:, :, :, 0:D]
                    for which, dst in enumerate((q2, k2)):
                        ins = act.copy(dst.bitcast(F32R), src[:, which].unsqueeze(2).to_broadcast([P, H, 2, D]))
                    ins.then_inc(S["qk_hi"], 1)
                name = ("v", a, b)
                act.wait_ge(*ring.full(i, name))
                act.copy(v[:, b, :, :, 0:D], slot(name)[:, 0:2 * E].rearrange("p (x h d) -> p x h d", x=2, h=H))\
                   .then_inc(read_sem(name), 1)
                if b == 1:
                    negmax(i, a, 0)
                beside((f"heads{b}", a, 0))
                for g in range(3):
                    name = ("k", a, b, g)
                    act.wait_ge(*ring.full(i, name))
                    act.copy(kT[b][:, 2 * g:2 * g + 2, :], slot(name)[:, :].rearrange("p (g n) -> p g n", g=2))\
                       .then_inc(read_sem(name), 1)

            def negmax(i, a, b):
                name = ("negmax", a, b)
                act.wait_ge(*ring.full(i, name))
                act.wait_ge(neg_in, 64 * (4 * (i + 1) + 2 * a + b))
                act.copy(msT, slot(name)[0:4 * HP, 0:N]).then_inc(read_sem(name), 1)

            def exp(i, a, b, n):
                name = ("score", a, b, n)
                act.wait_ge(*ring.full(i, name))
                act.wait_ge(*at(i, "pv_done", 6 * (2 * a + b) + n // 2 - NPROB // 2))
                act.activation(prob[:, n % NPROB], slot(name)[:, :].rearrange("p (g n) -> p g n", g=2), ACT.Exp,
                               scale=float(D) ** -0.5).then_inc(read_sem(name), 1)

            def context(i, a, b, g):
                n = 3 * (2 * a + b) + g
                act.wait_ge(*at(i, "pv_done", 2 * n + 1))
                act.copy(cT[:, g * N:(g + 1) * N], ctx_bank[:, 0:N])\
                   .then_inc(S["cbank_read"], 1)

            def ffn(i, kind, c):
                if kind == "split":
                    split_hi(i, c)
                if kind == "up":
                    name, e, m = ("up", c), c // MT, c % MT
                    act.wait_ge(*hid.full(i, name))
                    act.wait_ge(*at(i, "down_done", c - 2))
                    bias = keep["b1"][:, e * MT + m:e * MT + m + 1]
                    act.activation(gh[:, c % 2], slot(name)[:, :], ACT.Gelu, bias=bias)
                    act.wait_ge(*at(i, "gl_done", c - 1))
                    act.activation(gel, slot(name)[:, :], ACT.Gelu, bias=bias).then_inc(read_sem(name), 1)
                if kind == "gate":
                    prime(ACT.Exp, 5)
                    act.wait_ge(*at(i, "gate_chain", 1))
                    act.activation(ex[:, :, :], ex[:, :, :], ACT.Exp).then_inc(S["gate_exp"], 1)
                    prime(ACT.Gelu, 6)

            def attention(i, beside):
                for a in range(2):
                    beside_all(beside, a, "start", "chain1", "chain2")
                    split_hi(i, a)
                    beside(("parts", a, 0))
                    prepare(i, a, 0, beside)
                    beside_all(beside, a, "ready", "max0")
                    prepare(i, a, 1, beside)
                    beside(("next", a, 0))
                    beside(("both", a, 0))
                    prime(ACT.Exp, 1 + a)
                    for b in range(2):
                        for n in range(12):
                            exp(i, a, b, n)
                            if n in (5, 9):
                                context(i, a, b, n // 4 - 1)
                            if b == 0 and n == NEG_AT:
                                negmax(i, a, 1)
                        if b == 1:
                            prime(ACT.Gelu, 3 + a)
                        context(i, a, b, 2)
                    beside_all(beside, a, "mid", "exp1", "end")
                for k, rows in enumerate((P, E2)):
                    act.wait_ge(*ring.full(i, ("ctxT", k)))
                    act.copy(ctxT[k][0:rows, :], slot(("ctxT", k))[0:rows, :])\
                       .then_inc(read_sem(("ctxT", k)), 1)
                beside(("proj", 1, 0))
                beside(("over", 1, 0))

            pipeline(act, attention, ffn)

        @block.vector
        def _(dve):
            credit(dve, "ln_chain", "ln4_chain", "ln_affine", "ln4_affine", "ln_out", "ln4_out", "h_sum", "neg_hi", "neg_done",
                   "rs_done", "acc_read", "gate_chain")
            for plan in (ring, hid):
                for s, n in zip(plan.read_sem, plan.per):
                    dve.sem_inc(s, n)

            def statistics(after, tiles):
                st, mv, ve, yn, hv, sh = tiles
                dve.sem_inc(passed, 1)
                for blk in range(NBLK):
                    ins = dve.bn_aggr(mv[:, blk, :], st[:, blk, :])
                after(ins)
                after(dve.tensor_scalar(ve[:, :], mv[:, :, 1], EPS, None, ALU.add))
                after(dve.tensor_scalar(hv[:, :], ve[:, :], -0.5, None, ALU.mult), wait=False)
                after(dve.tensor_scalar(sh[:, :], ve[:, :].bitcast(I32), 1, None, ALU.logical_shift_right))
                after(dve.tensor_scalar(yn[:, :].bitcast(I32), sh[:, :], -1.0, MAGIC, ALU.mult, ALU.add))

            def norm(i, k, src, dst, gamma=None, beta=None, early=0):
                name, k0 = "ln_chain", k % 4
                done, step = S[name], iter(range(CHAIN * k0, CHAIN * (k0 + 1)))
                mv, yn = (mv4, yn4) if k == 4 else (mv1, yn1)

                def after(ins, wait=True):
                    ins.then_inc(done, 1)
                    event = next(step)
                    if wait:
                        dve.wait_ge(*at(i, name, event))

                if k < 4:
                    for blk in range(early, NBLK):
                        if k == 1:
                            dve.wait_ge(*at(i, "y_sum", blk))
                        ins = dve.bn_stats(st[:, blk, :], src[:, blk, :])
                    after(ins)
                    statistics(after, (st, mv, ve, yn, hv, sh))
                    for _ in range(NEWTON):
                        after(dve.tensor_tensor(tn[:, :], yn[:, :], yn[:, :], ALU.mult))
                        after(dve.tensor_tensor(tn[:, :], tn[:, :], hv[:, :], ALU.mult))
                        after(dve.scalar_tensor_tensor(out=yn[:, :], in0=tn[:, :], scalar=1.5, in1=yn[:, :],
                                                       op0=ALU.add, op1=ALU.mult))
                if gamma is None:
                    for blk in range(NBLK):
                        ins = dve.tensor_scalar(dst[:, blk], src[:, blk], mv[:, blk, 0:1], yn[:, blk:blk + 1],
                                                ALU.subtract, ALU.mult)
                else:
                    for blk in range(NBLK):
                        ins = dve.scalar_tensor_tensor(out=dst[:, blk], in0=src[:, blk], scalar=mv[:, blk, 0:1],
                                                       in1=gamma[:, :], op0=ALU.subtract, op1=ALU.mult)
                    affine = "ln4_affine" if k == 4 else "ln_affine"
                    ins.then_inc(S[affine], 1)
                    dve.wait_ge(*at(i, affine, k0 // 2))
                    for blk in range(NBLK):
                        ins = dve.scalar_tensor_tensor(out=dst[:, blk], in0=dst[:, blk], scalar=yn[:, blk:blk + 1],
                                                       in1=beta[:, :], op0=ALU.mult, op1=ALU.add)
                name = "ln4_out" if k == 4 else "ln_out"
                ins.then_inc(S[name], 1)
                dve.wait_ge(*at(i, name, k0))

            def split_lo(i, s):
                xh, xl, xch, xcl = xparts[s // 2]
                for k, (name, hi, lo, rows) in enumerate(((("split_a", s), xh, xl, P), (("split_c", s), xch, xcl, E2))):
                    dve.wait_ge(*at(i, "fhi_copy" if s >= 2 else "hi_copy", 2 * (s % 2) + k))
                    dve.tensor_tensor(lo[:, :], slot(name)[0:rows, :], hi[0:rows, :].bitcast(F32), ALU.subtract)\
                       .then_inc(read_sem(name), 1)

            def prepare(i, a, b, beside):
                for half in range(2):
                    name = ("qk", a, b, half)
                    dve.wait_ge(*at(i, "qk_hi", 2 * (2 * a + b) + half))
                    src = slot(name)[:, 0:2 * E].rearrange("p (x h d) -> p x h d", x=2, h=H)
                    dve.tensor_tensor(qs[:, half, :, 2 * D:3 * D].bitcast(F32R), src[:, 0], qs[:, half, :, 0:D],
                                      ALU.subtract)
                    dve.tensor_tensor(ks[:, half, :, D:2 * D].bitcast(F32R), src[:, 1], ks[:, half, :, 0:D],
                                      ALU.subtract).then_inc(read_sem(name), 1)
                beside((f"heads{b}", a, 0))
                for g in range(3):
                    name = ("q", a, b, g)
                    dve.wait_ge(*ring.full(i, name))
                    dve.tensor_copy(qT[b][:, 2 * g:2 * g + 2, :], slot(name)[:, :].rearrange("p (g n) -> p g n", g=2))\
                       .then_inc(read_sem(name), 1)

            def maximum(i, a, b, n):
                name = ("max", a, b, n)
                dve.wait_ge(*ring.full(i, name))
                dve.tensor_reduce(mx[:, n // HP, n % 2, n % HP // 2 * 2:n % HP // 2 * 2 + 2],
                                  slot(name)[:, :].rearrange("p (g n) -> p g n", g=2),
                                  AX.X, ALU.max).then_inc(read_sem(name), 1)

            def negate(i, a, b):
                for n in (9, 10, 11):
                    dve.wait_ge(*ring.read(i, ("max", a, b, n)))
                dve.tensor_scalar(ms[:, :, :, 0, :], mx[:, :, :, :], -1.0, None, ALU.mult).then_inc(S["neg_hi"], 1)
                dve.wait_ge(*at(i, "neg_hi", 2 * a + b))
                for half in range(2):
                    ins = dve.scalar_tensor_tensor(out=ms[:, half, :, 1, :], in0=mx[:, half], scalar=-1.0,
                                                   in1=ms[:, half, :, 0, :].bitcast(F32), op0=ALU.mult,
                                                   op1=ALU.subtract)
                ins.then_inc(S["neg_done"], 1)

            def context(i, a, b):
                for half in range(2):
                    name = ("ctx", a, b, half)
                    dve.wait_ge(*ring.full(i, name))
                    src = slot(name)[:, 0:3 * P].rearrange("p (h d) -> p h d", d=2 * D)
                    dve.reciprocal(rsum[:, half, :], src[:, :, D]).then_inc(S["rs_done"], 1)
                    dve.wait_ge(*at(i, "rs_done", 2 * (2 * a + b) + half))
                    dve.tensor_tensor(y[:, 2 * b + half, :].rearrange("p (h d) -> p h d", d=D), src[:, :, 0:D],
                                      rsum[:, half, :].unsqueeze(2).to_broadcast([P, H, D]), ALU.mult)\
                       .then_inc(read_sem(name), 1)

            def gate(i):
                chain, step = S["gate_chain"], iter(range(12))

                def after(ins, wait=True):
                    ins.then_inc(chain, 1)
                    event = next(step)
                    if wait:
                        dve.wait_ge(*at(i, "gate_chain", event))

                dve.wait_ge(*full(i, ("gate",)))
                dve.tensor_copy(lg[:, :, :], slot(("gate",))[:, 0:NBLK * NEXP].rearrange("p (c e) -> p c e", c=NBLK))\
                   .then_inc(read_sem(("gate",)), 1)
                dve.wait_ge(*read(i, ("gate",)))
                l_j = lg[:, :, :].unsqueeze(2).to_broadcast([P, NBLK, NEXP, NEXP])
                l_e = lg[:, :, :].unsqueeze(3).to_broadcast([P, NBLK, NEXP, NEXP])
                after(dve.tensor_reduce(m1[:, :], lg[:, :, :], AX.X, ALU.max))
                after(dve.tensor_tensor(ex[:, :, :], lg[:, :, :],
                                        m1[:, :].unsqueeze(2).to_broadcast([P, NBLK, NEXP]), ALU.subtract),
                      wait=False)
                after(dve.tensor_tensor(gt4[:, :, :, :], l_j, l_e, ALU.is_gt), wait=False)
                after(dve.tensor_tensor(eq4[:, :, :, :], l_j, l_e, ALU.is_equal))
                after(dve.tensor_tensor(eq4[:, :, :, :], eq4[:, :, :, :],
                                        keep["tri"][:, :, :].unsqueeze(1).to_broadcast([P, NBLK, NEXP, NEXP]),
                                        ALU.mult))
                after(dve.tensor_tensor(gt4[:, :, :, :], gt4[:, :, :, :], eq4[:, :, :, :], ALU.add))
                after(dve.tensor_reduce(rank[:, :, :], gt4[:, :, :, :], AX.X, ALU.add))
                after(dve.tensor_scalar(rank[:, :, :], rank[:, :, :], 1.5, None, ALU.is_lt))
                dve.wait_ge(*at(i, "gate_exp", 0))
                after(dve.tensor_tensor(ex[:, :, :], ex[:, :, :], rank[:, :, :], ALU.mult))
                after(dve.tensor_reduce(s1[:, :], ex[:, :, :], AX.X, ALU.add))
                after(dve.reciprocal(s1[:, :], s1[:, :]))
                after(dve.tensor_tensor(comb[:, :, :], ex[:, :, :],
                                        s1[:, :].unsqueeze(2).to_broadcast([P, NBLK, NEXP]), ALU.mult))

            def expert_sum(i, e):
                if e == 1:
                    dve.wait_ge(*at(i, "res", 0))
                dve.wait_ge(*at(i, "down_done", MT * (e + 1) - 1))
                dve.wait_ge(*at(i, "acc_read", e - 1))
                for blk in range(NBLK):
                    src = mlp_bank[blk // 2][:, (blk % 2) * E:(blk % 2 + 1) * E]
                    ins = dve.scalar_tensor_tensor(out=x[:, blk], in0=src, scalar=comb[:, blk, e - 1:e],
                                                   in1=x[:, blk], op0=ALU.mult, op1=ALU.add)
                ins.then_inc(S["acc_read"], 1)

            def ffn(i, kind, c):
                if kind == "split":
                    split_lo(i, c)
                if kind == "sum":
                    dve.wait_ge(stored, 16 * i + 16)
                    dve.wait_ge(*at(i, "down_done", MT - 1))
                    for j in range(2):
                        ins = dve.tensor_tensor(x[:, 2 * j:2 * j + 2],
                                                mlp_bank[j][:, 0:2 * E].rearrange("p (c e) -> p c e", c=2),
                                                y[:, 2 * j:2 * j + 2], ALU.add)
                    ins.then_inc(S["acc_read"], 1)
                if kind == "stats":
                    step = iter(range(6))

                    def after(ins, wait=True):
                        ins.then_inc(S["ln4_chain"], 1)
                        event = next(step)
                        if wait:
                            dve.wait_ge(*at(i, "ln4_chain", event))

                    dve.wait_ge(*at(i, "acc_read", 0))
                    for blk in range(NBLK):
                        ins = dve.bn_stats(st[:, blk, :], x[:, blk, :])
                    after(ins)
                    statistics(after, (st, mv4, ve, yn4, hv4, sh))
                if kind == "norm":
                    dve.wait_ge(*at(i, "ln_pool", 4 * NEWTON - 1))
                    norm(i, 4, x, xm, keep["ln_g4"], keep["ln_b4"])
                if kind == "gate":
                    gate(i)
                if kind == "up" and c % MT == 1 and c > 2 * MT:
                    expert_sum(i, c // MT - 1)
                if kind == "last":
                    expert_sum(i, NEXP)

            def attention(i, beside):
                for a in range(2):
                    if a == 0:
                        beside(("start", 0, 0))
                        dve.wait_ge(u_in, 16 * i + 16)
                        norm(i, 0, fresh, u)
                    split_lo(i, a)
                    beside(("parts", a, 0))
                    prepare(i, a, 0, beside)
                    beside(("ready", a, 0))
                    for n in range(12):
                        maximum(i, a, 0, n)
                        if n % 3 == 2:
                            beside(("max0", a, n // 3))
                    negate(i, a, 0)
                    prepare(i, a, 1, beside)
                    beside(("next", a, 0))
                    for n in range(12):
                        maximum(i, a, 1, n)
                        if n == LAG:
                            beside(("both", a, 0))
                    negate(i, a, 1)
                    beside(("mid", a, 0))
                    context(i, a, 0)
                    beside(("exp1", a, 0))
                    if a == 0:
                        for blk in range(2):
                            dve.wait_ge(*at(i, "y_sum", blk))
                            dve.bn_stats(st[:, blk, :], y[:, blk, :])
                    context(i, a, 1)
                    beside(("end", a, 0))
                    if a == 0:
                        beside(("start", 1, 0))
                        norm(i, 1, y, y, keep["ln_g1"], keep["ln_b1"], early=2)
                        dve.wait_ge(h_in, 16 * i + 16)
                        dve.tensor_tensor(h[:, :, :], h[:, :, :], y[:, :, :], ALU.add).then_inc(S["h_sum"], 1)
                        dve.wait_ge(*at(i, "h_sum", 0))
                        beside(("chain1", 1, 0))
                        norm(i, 2, h, u)
                        beside(("chain2", 1, 0))
                        norm(i, 3, u, y, keep["ln_g3"], keep["ln_b3"])
                beside(("proj", 1, 0))
                for j in range(2):
                    name = ("proj", j)
                    dve.wait_ge(*ring.full(i, name))
                    dve.tensor_tensor(y[:, 2 * j:2 * j + 2], slot(name)[:, 0:2 * E].rearrange("p (c e) -> p c e", c=2),
                                      u[:, 2 * j:2 * j + 2], ALU.add).then_inc(read_sem(name), 1)
                beside(("over", 1, 0))

            pipeline(dve, attention, ffn)

        @block.tensor
        def _(pe):
            credit(pe, "pv_done", "down_done")
            for plan in (ring, hid):
                for s, n in zip(plan.full_sem, plan.per):
                    pe.sem_inc(s, n)

            def split(i, s, src):
                pe.wait_ge(*room(i, ("split_c", s)))
                name = ("split_a", s)
                pe.wait_ge(*room(i, name))
                for blk in range(NBLK):
                    mm = pe.transpose(slot(name)[:, blk * P:(blk + 1) * P], src[:, blk, 0:P], ident[:, :])
                mm.then_inc(full_sem(name), 1)
                name = ("split_c", s)
                for blk in range(NBLK):
                    mm = pe.transpose(slot(name)[0:E2, blk * P:(blk + 1) * P], src[:, blk, P:E], ident[:, :])
                mm.then_inc(full_sem(name), 1)

            def bias_of(q, c0, c1):
                return keep["ones"][q:q + 2, :], keep["bias"][q:q + 2, c0:c1]

            def tokens_by(o, parts, blk, wh, wl, wc, bias):
                xh, xl, xch, xcl = parts
                t = slice(blk * P, (blk + 1) * P)
                pe.matmul(o, *bias, start=True, stop=False)
                pe.matmul(o, xh[:, t], wh, start=False, stop=False)
                pe.matmul(o, xh[:, t], wl, start=False, stop=False)
                pe.matmul(o, xl[:, t], wh, start=False, stop=False)
                pe.matmul(o, xch[:, t], wc, start=False, stop=False)
                return pe.matmul(o, xcl[:, t], wc[0:E2], start=False, stop=True)

            def prepare(i, a, b, beside):
                wh, wl, wc = (keep[k][:, a] for k in ("wq_h", "wq_l", "wq_c"))
                for half in range(2):
                    name = ("qk", a, b, half)
                    pe.wait_ge(*ring.room(i, name))
                    tokens_by(slot(name)[:, 0:2 * E], xparts[0], 2 * b + half, wh[:, 0:2 * E], wl[:, 0:2 * E],
                              wc[:, 0:2 * E], bias_of(BIAS_AT[a], 0, 2 * E)).then_inc(full_sem(name), 1)
                name = ("v", a, b)
                pe.wait_ge(*ring.room(i, name))
                for half in range(2):
                    mm = tokens_by(slot(name)[:, half * E:(half + 1) * E], xparts[0], 2 * b + half, wh[:, 2 * E:],
                                   wl[:, 2 * E:], wc[:, 2 * E:], bias_of(BIAS_AT[a], 2 * E, 3 * E))
                mm.then_inc(full_sem(name), 1)
                if b == 1:
                    negmax(i, a, 0)
                beside((f"heads{b}", a, 0))
                for half in range(2):
                    pe.wait_ge(*ring.read(i, ("qk", a, b, half)))
                for x_, src in (("k", ks), ("q", qs)):
                    for g in range(3):
                        name = (x_, a, b, g)
                        pe.wait_ge(*ring.room(i, name))
                        for k in range(4):
                            hp, half = 2 * g + k // 2, k % 2
                            mm = pe.transpose(slot(name)[:, k * P:(k + 1) * P],
                                              src[:, half, 2 * hp:2 * hp + 2, :].rearrange("p h d -> p (h d)"),
                                              ident[:, :])
                        mm.then_inc(full_sem(name), 1)

            def maximum(i, a, b, n):
                name, half, g, p = ("max", a, b, n), n // HP, n % HP // 2, n % 2
                r = slice(64 * p, 64 * p + 3 * D)
                if n == 0:
                    for k in range(3):
                        pe.wait_ge(*ring.read(i, ("q", a, b, k)))
                pe.wait_ge(*ring.room(i, name))
                for k in range(2):
                    mm = pe.matmul(slot(name)[:, k * N:(k + 1) * N], qT[b][r, 2 * g + k, half * P:(half + 1) * P],
                                   kT[b][r, 2 * g + k, :], start=True, stop=True)
                mm.then_inc(full_sem(name), 1)

            def negmax(i, a, b):
                name = ("negmax", a, b)
                pe.wait_ge(*at(i, "neg_done", 2 * a + b))
                pe.wait_ge(*ring.room(i, name))
                for half in range(2):
                    mm = pe.transpose(slot(name)[0:4 * HP, half * P:(half + 1) * P],
                                      ms[:, half].rearrange("p a r h -> p (a r h)").bitcast(F32), ident[:, :])
                mm.then_inc(full_sem(name), 1)

            def score(i, a, b, n):
                name, g, kb, p = ("score", a, b, n), n // 4, n // 2 % 2, n % 2
                r = slice(64 * p, 64 * p + 3 * D + 2)
                if n == 0:
                    pe.wait_ge(neg_in, 64 * (4 * (i + 1) + 2 * a + b + 1))
                pe.wait_ge(*ring.room(i, name))
                for k in range(2):
                    mm = pe.matmul(slot(name)[:, k * N:(k + 1) * N], kT[b][r, 2 * g + k, kb * P:(kb + 1) * P],
                                   qT[b][r, 2 * g + k, :], start=True, stop=True)
                mm.then_inc(full_sem(name), 1)

            def pv(i, a, b, w):
                g, kb = w // 2, w % 2
                n = 3 * (2 * a + b) + g
                if w == 0:
                    pe.wait_ge(*ring.read(i, ("v", a, b)))
                if kb == 0:
                    pe.wait_ge(*at(i, "cbank_read", n - 1))
                for k in range(2):
                    pe.wait_ge(*ring.read(i, ("score", a, b, 2 * w + k)))
                for j in range(4):
                    mm = pe.matmul(ctx_bank[32 * j:32 * j + 32, 0:N],
                                   v[:, b, kb, 4 * g + j, :], prob[:, (2 * w + j % 2) % NPROB, j // 2, :],
                                   start=(kb == 0), stop=(kb == 1))
                mm.then_inc(S["pv_done"], 1)

            def context(i, a, b):
                pe.wait_ge(*at(i, "cbank_read", 3 * (2 * a + b) + 2))
                for half in range(2):
                    name = ("ctx", a, b, half)
                    pe.wait_ge(*ring.room(i, name))
                    for g in range(3):
                        mm = pe.transpose(slot(name)[:, g * P:(g + 1) * P],
                                          cT[:, g * N + half * P:g * N + (half + 1) * P], ident[:, :])
                    mm.then_inc(full_sem(name), 1)

            def up(i, c):
                name, e, m = ("up", c), c // MT, c % MT
                xh, xl, xch, xcl = xparts[1]
                w = slice(m * P, (m + 1) * P)
                if c == 0:
                    pe.wait_ge(*read(i, ("split_c", 2)))
                pe.wait_ge(*room(i, name))
                o = slot(name)[:, :]
                wh, wl, wc = keep["w1_h"][:, e, w], keep["w1_l"][:, e, w], keep["w1_c"][:, e, w]
                pe.matmul(o, wh, xh[:, :], start=True, stop=False)
                pe.matmul(o, wh, xl[:, :], start=False, stop=False)
                pe.matmul(o, wl, xh[:, :], start=False, stop=False)
                pe.matmul(o, wc, xch[:, :], start=False, stop=False)
                pe.matmul(o, wc[0:E2], xcl[:, :], start=False, stop=True).then_inc(full_sem(name), 1)

            def down(i, c):
                e, m = c // MT, c % MT
                o = [mlp_bank[blk // 2][:, (blk % 2) * E:(blk % 2 + 1) * E] for blk in range(NBLK)]
                if m == 0:
                    pe.wait_ge(*at(i, "acc_read", e - 1))
                    for blk in range(NBLK):
                        pe.matmul(o[blk], *bias_of(BIAS_AT[2], e * E, (e + 1) * E), start=(blk % 2 == 0), stop=False,
                                  skip_group_check=True)
                pe.wait_ge(*at(i, "gl_done", c))
                wh, wl = keep["w2_h"][:, e, m * E:(m + 1) * E], keep["w2_l"][:, e, m * E:(m + 1) * E]
                for blk in range(NBLK):
                    t = slice(blk * P, (blk + 1) * P)
                    for k, (g_, w) in enumerate(((gh, wh), (gh, wl), (gl, wh))):
                        mm = pe.matmul(o[blk], g_[:, c % 2, t], w, start=False, stop=(m == MT - 1 and k == 2),
                                       skip_group_check=True)
                mm.then_inc(S["down_done"], 1)

            def gate(i):
                name = ("gate",)
                pe.wait_ge(*read(i, ("split_c", 3)))
                pe.wait_ge(*room(i, name))
                for blk in range(NBLK):
                    mm = tokens_by(slot(name)[:, blk * NEXP:(blk + 1) * NEXP], xparts[1], blk, keep["gw_h"][:, :],
                                   keep["gw_l"][:, :], keep["gw_c"][:, :],
                                   bias_of(BIAS_AT[2], NMLP * E, NMLP * E + NEXP))
                mm.then_inc(full_sem(name), 1)

            def ffn(i, kind, c):
                if kind == "split":
                    if c == 2:
                        for j in range(2):
                            pe.wait_ge(*ring.read(i, ("proj", j)))
                    else:
                        pe.wait_ge(*at(i, "ln4_out", 0))
                    split(i, c, y if c == 2 else xm)
                if kind == "up":
                    up(i, c)
                if kind == "down":
                    down(i, c)
                if kind == "gate":
                    gate(i)

            def attention(i, beside):
                for a in range(2):
                    beside_all(beside, a, "start", "chain1", "chain2")
                    pe.wait_ge(*at(i, "ln_out", 3 * a))
                    split(i, a, u if a == 0 else y)
                    beside(("parts", a, 0))
                    for part in "ac":
                        pe.wait_ge(*ring.read(i, ("split_" + part, a)))
                    prepare(i, a, 0, beside)
                    beside(("ready", a, 0))
                    for n in range(12):
                        maximum(i, a, 0, n)
                        if n % 3 == 2:
                            beside(("max0", a, n // 3))
                    prepare(i, a, 1, beside)
                    beside(("next", a, 0))
                    for n in range(12 + LAG):
                        if n < 12:
                            maximum(i, a, 1, n)
                        if n == LAG:
                            beside(("both", a, 0))
                        if n >= LAG:
                            score(i, a, 0, n - LAG)
                            if (n - LAG) % 2 and n - LAG >= 3:
                                pv(i, a, 0, (n - LAG - 3) // 2)
                        if n == NEG_AT + LAG:
                            negmax(i, a, 1)
                    pv(i, a, 0, 5)
                    beside(("mid", a, 0))
                    context(i, a, 0)
                    for n in range(12):
                        score(i, a, 1, n)
                        if n % 2 and n >= 3:
                            pv(i, a, 1, (n - 3) // 2)
                        if n == 2:
                            beside(("exp1", a, 0))
                    pv(i, a, 1, 5)
                    context(i, a, 1)
                    beside(("end", a, 0))
                for half in range(2):
                    pe.wait_ge(*ring.read(i, ("ctx", 1, 1, half)))
                for k in (1, 0):
                    pe.wait_ge(*ring.room(i, ("ctxT", k)))
                for k, c0, c1 in ((0, 0, P), (1, P, E)):
                    name = ("ctxT", k)
                    for blk in range(NBLK):
                        mm = pe.transpose(slot(name)[0:c1 - c0, blk * P:(blk + 1) * P], y[:, blk, c0:c1], ident[:, :])
                    mm.then_inc(full_sem(name), 1)
                beside(("proj", 1, 0))
                for k in range(2):
                    pe.wait_ge(*ring.read(i, ("ctxT", k)))
                for j in range(2):
                    name = ("proj", j)
                    pe.wait_ge(*ring.room(i, name))
                    for k in range(2):
                        blk = 2 * j + k
                        o = slot(name)[:, k * E:(k + 1) * E]
                        pe.matmul(o, *bias_of(BIAS_AT[0], 3 * E, 4 * E), start=True, stop=False)
                        pe.matmul(o, ctxT[0][:, blk * P:(blk + 1) * P], keep["ow_a"][:, :], start=False, stop=False)
                        mm = pe.matmul(o, ctxT[1][0:E2, blk * P:(blk + 1) * P], keep["ow_c"][:, :],
                                       start=False, stop=True)
                    mm.then_inc(full_sem(name), 1)
                beside(("over", 1, 0))

            pipeline(pe, attention, ffn)


def build(nc, a, out):
    const = {
        "scratch1": nc.dram_tensor("scratch1", [B, L1 * GP, C1], F32, kind="Internal").ap(),
        "scratch2": nc.dram_tensor("scratch2", [B, L2 * GP, C2], F32, kind="Internal").ap(),
        "h": nc.dram_tensor("h_tokens", [B * N, E], F32, kind="Internal").ap(),
    }
    shapes = {
        "ident": ([P, P], F32), "ones": ([P, P], F32R), "b1": ([P, NMLP * MT], F32), "tri": ([P, NEXP, NEXP], F32),
        "wq_h": ([P, 2, 3 * E], F32R), "wq_l": ([P, 2, 3 * E], F32R), "wq_c": ([P, 2, 3 * E], F32R),
        "bias": ([P, NMLP * E + NEXP], F32R), "gw_h": ([P, NEXP], F32R), "gw_l": ([P, NEXP], F32R),
        "gw_c": ([P, NEXP], F32R),
        "w1_h": ([P, NMLP, HID], F32R), "w1_l": ([P, NMLP, HID], F32R), "w1_c": ([P, NMLP, HID], F32R),
        "w2_h": ([P, NMLP, MT * E], F32R), "w2_l": ([P, NMLP, MT * E], F32R),
        "ow_a": ([P, E], F32), "ow_c": ([E2, E], F32),
        "ln_g1": ([P, E], F32), "ln_b1": ([P, E], F32), "ln_g3": ([P, E], F32), "ln_b3": ([P, E], F32),
        "ln_g4": ([P, E], F32), "ln_b4": ([P, E], F32),
    }
    with ExitStack() as ctx:
        keep = {name: ctx.enter_context(nc.sbuf_tensor("keep_" + name, shape, dt))
                for name, (shape, dt) in shapes.items()}
        prepare_and_tokenize(nc, a, keep, const)
        tower(nc, keep, const, out)


def interpolation(length):
    pos = (np.arange(N, dtype=np.float32) + np.float32(0.5)) * np.float32(length / N) - np.float32(0.5)
    pos = np.clip(pos, 0.0, length - 1).astype(np.float32)
    i0 = np.floor(pos).astype(np.int64)
    i1 = np.minimum(i0 + 1, length - 1)
    w = (pos - i0).astype(np.float32)
    m = np.zeros((length, N), np.float32)
    m[i0, np.arange(N)] += np.float32(1.0) - w
    m[i1, np.arange(N)] += w
    return m


def kernel(**inputs):
    import concourse.bacc as bacc
    from concourse.bass_utils import run_bass_kernel_spmd

    t = {k: np.asarray(v) for k, v in inputs.items()}
    g = lambda name: t["L0_" + name]
    xin = t["x"]
    put = {}
    for k, p in enumerate(PRE):
        n = IMG // p
        put[f"x{k}r"] = xin.reshape(B, CH, n, p, n, p).transpose(2, 4, 0, 3, 5, 1).reshape(n * n, B * CH * p * p)
        if p == 1:
            put["x0r"] = xin.transpose(2, 3, 1, 0).reshape(n * n, CH * B)
    put["idx0"] = g("tok_idx0").reshape(2, P, GP).transpose(1, 0, 2)
    put["idx1"] = g("tok_idx1").reshape(8, P).T
    put["idx2"] = g("tok_idx2").reshape(2, P).T
    put["w0T"] = g("tok_W0").T
    put["w1T"] = g("tok_W1").T.reshape(2, 96, EMB).transpose(1, 0, 2)
    put["w2T"] = g("tok_W2").T.reshape(6, P, EMB).transpose(1, 0, 2)
    put["wfT"] = g("tok_Wf").T.reshape(3, EMB, E).transpose(1, 0, 2)
    put["tb"] = np.stack([g("tok_b0"), g("tok_b1"), g("tok_b2")], 1)
    put["bf"] = g("tok_bf")
    put["interp1"] = interpolation(L1)
    m2, two = interpolation(L2), np.zeros((4, 2, L2, 2, N), np.float32)
    for r in range(2):
        two[:, r, :, r, :] = m2
    put["interp2"] = two.reshape(P, 2, N)
    put["wqkv"] = np.stack([g("attn_w_qkv"), g("ffn_in_w").T])
    put["bqkv"] = np.stack([g("attn_b_qkv"), g("ffn_in_b")])
    put["g1"], put["be1"] = g("attn_ln_gamma"), g("attn_ln_beta")
    put["g3"], put["be3"] = g("ffn_ln1_g"), g("ffn_ln1_b")
    put["g4"], put["be4"] = g("ffn_ln2_g"), g("ffn_ln2_b")
    put["owT"], put["ob"] = g("ffn_out_w").T, g("ffn_out_b").reshape(1, E)
    put["gate_wT"], put["gate_b"] = g("ffn_gate_w").T, g("ffn_gate_b").reshape(1, NEXP)
    put["w1"] = np.concatenate([g("ffn_mlp_w1")[None], g("ffn_exp_w1")])
    put["b1"] = np.concatenate([g("ffn_mlp_b1")[None], g("ffn_exp_b1")]).reshape(NMLP * MT, P).T
    w2 = np.concatenate([g("ffn_mlp_w2")[None], g("ffn_exp_w2")])
    put["w2"] = w2.reshape(NMLP, MT, P, E).transpose(2, 0, 1, 3).reshape(P, NMLP, MT * E)
    put["b2"] = np.concatenate([g("ffn_mlp_b2")[None], g("ffn_exp_b2")]).reshape(1, NMLP * E)
    put["tri"] = np.tril(np.ones((NEXP, NEXP), np.float32), -1)

    nc = bacc.Bacc("TRN2", target_bir_lowering=False, num_devices=1)
    put = {k: np.ascontiguousarray(v) for k, v in put.items()}
    aps = {k: nc.dram_tensor("in_" + k, v.shape, mybir.dt.from_np(v.dtype), kind="ExternalInput").ap()
           for k, v in put.items()}
    out = nc.dram_tensor("out", (B, N, E), F32, kind="ExternalOutput").ap()
    build(nc, aps, out)
    r = run_bass_kernel_spmd(nc, [{"in_" + k: v for k, v in put.items()}], core_ids=[0])
    return r.results[0]["out"]
```
